# Optimizing a Trainium2 kernel written in Bass

```python
import numpy as np
import jax
import jax.numpy as jnp

def _softmax(x, axis=-1):
    return jax.nn.softmax(x, axis=axis)

def _gelu(x):
    return jax.nn.gelu(x, approximate=True)

def _silu(x):
    return jax.nn.silu(x)

def _sigmoid(x):
    return jax.nn.sigmoid(x)

def _layernorm(x, axis=-1, eps=1e-05):
    m = jnp.mean(x, axis=axis, keepdims=True)
    v = jnp.var(x, axis=axis, keepdims=True)
    return (x - m) / jnp.sqrt(v + eps)

def _scatter_add(tgt, idx, src, axis=0):
    return tgt.at[idx].add(src)

def _segment_sum(src, seg, n):
    return jax.ops.segment_sum(src, seg, n)
kernel_name = 'mk_gnn_ffn_d1_gnn_r8_6a3e82'

def setup_inputs(seed: int=0):
    np.random.seed(seed)
    _w = jnp.asarray

    def _rec_inputs():
        import jax
        import jax.numpy as jnp
        _gk = jax.random.key(seed)
        x = -0.0003713 + 1 * jax.random.normal(jax.random.fold_in(_gk, 1), (6250, 256), jnp.float32)
        src = jax.random.randint(jax.random.fold_in(_gk, 2), (200000,), 0, 6250, jnp.int32)
        dst = jax.random.randint(jax.random.fold_in(_gk, 3), (200000,), 0, 6250, jnp.int32)
        _o = jnp.argsort(dst, stable=True)
        src = src[_o]
        dst = dst[_o]
        edge_attr_16 = -0.00010739 + 0.99994 * jax.random.normal(jax.random.fold_in(_gk, 12), (200000, 16), jnp.float32)
        edge_attr_4 = jax.random.uniform(jax.random.fold_in(_gk, 13), (200000, 4), jnp.float32, 0.0, 1)
        return (x, src, dst, edge_attr_16, edge_attr_4)
    x, src, dst, edge_attr_16, edge_attr_4 = _rec_inputs()

    def _L0_gnn_setup():
        import jax, jax.numpy as jnp
        import numpy as np
        N = 6250
        E = 100000
        IN_DIM = 256
        H = 8
        D = 32
        T = 4
        F = 16
        NEG_SLOPE = 0.2
        key = jax.random.key(seed)
        ks = jax.random.split(key, 9)
        feat = jax.random.normal(ks[0], (N, IN_DIM), dtype=jnp.float32)
        e_pro = jax.random.normal(ks[1], (E, F), dtype=jnp.float32)
        mask = jax.random.uniform(ks[2], (E, T), dtype=jnp.float32)
        W_n = jax.random.normal(ks[3], (IN_DIM, H * D), dtype=jnp.float32) * (1.0 / np.sqrt(IN_DIM))
        attn_l = jax.random.normal(ks[4], (H, D, T), dtype=jnp.float32) * 0.1
        attn_r = jax.random.normal(ks[5], (H, D, T), dtype=jnp.float32) * 0.1
        attn_m = jax.random.normal(ks[6], (H, F, T), dtype=jnp.float32) * 0.1
        src = jax.random.randint(ks[7], (E,), 0, N, dtype=jnp.int32)
        dst = jax.random.randint(ks[8], (E,), 0, N, dtype=jnp.int32)
        return {'feat': feat, 'e_pro': e_pro, 'mask': mask, 'W_n': W_n, 'attn_l': attn_l, 'attn_r': attn_r, 'attn_m': attn_m, 'src': src, 'dst': dst}
    _L0_gnn_all = _L0_gnn_setup()
    _L0_gnn_in = {k: v for k, v in _L0_gnn_all.items() if k in ('W_n', 'attn_l', 'attn_r', 'attn_m')}
    del _L0_gnn_all

    def _L0_ffn_setup():
        import jax, jax.numpy as jnp
        import numpy as np
        N_EXPERTS = 8
        TOP_K = 2
        key = jax.random.key(seed)
        ks = jax.random.split(key, 5)
        B, T, C, E, H = (8, 256, 256, 8, 682)
        scale = 1.0 / np.sqrt(C)
        return {'x': jax.random.normal(ks[0], (B, T, C), dtype=jnp.float32), 'router_w': jax.random.normal(ks[1], (E, C), dtype=jnp.float32) * scale, 'w1': jax.random.normal(ks[2], (E, H, C), dtype=jnp.float32) * scale, 'w2': jax.random.normal(ks[3], (E, C, H), dtype=jnp.float32) * (1.0 / np.sqrt(H)), 'w3': jax.random.normal(ks[4], (E, H, C), dtype=jnp.float32) * scale}
    _L0_ffn_all = _L0_ffn_setup()
    _L0_ffn_in = {k: v for k, v in _L0_ffn_all.items() if k in ('router_w', 'w1', 'w2', 'w3')}
    del _L0_ffn_all
    return {'x': x, 'src': src, 'dst': dst, 'edge_attr_16': edge_attr_16, 'edge_attr_4': edge_attr_4, 'L0_gnn_W_n': _L0_gnn_in['W_n'], 'L0_gnn_attn_l': _L0_gnn_in['attn_l'], 'L0_gnn_attn_r': _L0_gnn_in['attn_r'], 'L0_gnn_attn_m': _L0_gnn_in['attn_m'], 'L0_ffn_router_w': _L0_ffn_in['router_w'], 'L0_ffn_w1': _L0_ffn_in['w1'], 'L0_ffn_w2': _L0_ffn_in['w2'], 'L0_ffn_w3': _L0_ffn_in['w3']}

def reference(x, src, dst, edge_attr_16, edge_attr_4, L0_gnn_W_n, L0_gnn_attn_l, L0_gnn_attn_r, L0_gnn_attn_m, L0_ffn_router_w, L0_ffn_w1, L0_ffn_w2, L0_ffn_w3):
    import jax
    import jax.numpy as jnp

    def _L0_gnn_ref(feat, e_pro, mask, W_n, attn_l, attn_r, attn_m, src, dst):
        import jax, jax.numpy as jnp
        import numpy as np
        N = 6250
        E = 100000
        IN_DIM = 256
        H = 8
        D = 32
        T = 4
        F = 16
        NEG_SLOPE = 0.2
        feat_src = (feat @ W_n).reshape(N, H, D)
        el = jnp.einsum('nhd,hdt->nht', feat_src, attn_l)
        er = jnp.einsum('nhd,hdt->nht', feat_src, attn_r)
        em = jnp.einsum('ef,hft->eht', e_pro, attn_m)
        left = jnp.einsum('eht,et->eh', el[src], mask)
        right = jnp.einsum('eht,et->eh', er[dst], mask)
        em_e = jnp.einsum('eht,et->eh', em, mask)
        e = (left + right + em_e) / 3.0
        e = jnp.where(e > 0, e, NEG_SLOPE * e)
        e_max = jax.ops.segment_max(e, dst, num_segments=N)
        e_exp = jnp.exp(e - e_max[dst])
        e_sum = jax.ops.segment_sum(e_exp, dst, num_segments=N)
        a = e_exp / e_sum[dst]
        msg = feat_src[src] * a[:, :, None]
        rst = jax.ops.segment_sum(msg, dst, num_segments=N)
        return rst.reshape(N, H * D)

    def _L0_ffn_ref(x, router_w, w1, w2, w3):
        import jax, jax.numpy as jnp
        import numpy as np
        N_EXPERTS = 8
        TOP_K = 2
        B, T, C = x.shape
        flat = x.reshape(-1, C)
        logits = flat @ router_w.T
        probs = jax.nn.softmax(logits, axis=-1)
        topk_probs, topk_idx = jax.lax.top_k(probs, TOP_K)
        topk_probs = topk_probs / (jnp.sum(topk_probs, axis=-1, keepdims=True) + 1e-09)
        onehot = jax.nn.one_hot(topk_idx, N_EXPERTS, dtype=flat.dtype)
        gates = jnp.einsum('nk,nke->ne', topk_probs, onehot)
        h1 = jnp.einsum('nc,ehc->neh', flat, w1)
        h3 = jnp.einsum('nc,ehc->neh', flat, w3)
        h = jax.nn.silu(h1) * h3
        y = jnp.einsum('neh,ech->nec', h, w2)
        out = jnp.einsum('ne,nec->nc', gates, y)
        return out.reshape(B, T, C)
    x = x + _L0_gnn_ref(_layernorm(x, axis=-1), edge_attr_16, edge_attr_4, L0_gnn_W_n, L0_gnn_attn_l, L0_gnn_attn_r, L0_gnn_attn_m, src, dst)
    x = x + _L0_ffn_ref(_layernorm(x, axis=-1)[None], L0_ffn_router_w, L0_ffn_w1, L0_ffn_w2, L0_ffn_w3)[0]
    return x

_drawn_inputs = setup_inputs


def setup_inputs(seed=0):
    import zlib

    import numpy as np

    out = dict(_drawn_inputs(seed))
    spreads = {}
    factors = {}
    for name, (base, spread) in spreads.items():
        noise = np.random.default_rng([zlib.crc32(name.encode()), seed]).standard_normal(out[name].shape)
        drawn = base * np.exp(spread * noise) if base else spread * noise
        out[name] = jnp.asarray(drawn.astype(out[name].dtype))
    for name, factor in factors.items():
        out[name] = (out[name] * factor).astype(out[name].dtype)
    return out
```

```python
import concourse.bass as bass
from concourse import mybir
from contextlib import ExitStack


F32 = mybir.dt.float32
I32 = mybir.dt.int32
ALU = mybir.AluOpType
ACT = mybir.ActivationFunctionType
AX = mybir.AxisListType
ds = bass.ds

P = 128
NODES, DIM = 6250, 256
EDGES = 200000
HEADS, HDIM, T, F = 8, 32, 4, 16
HT = HEADS * T
EXPERTS, HID = 8, 682
SLOPE, LN_EPS = 0.2, 1e-5

BLOCKS = -(-NODES // P)
LAST = NODES - (BLOCKS - 1) * P
ROWS = BLOCKS * P
GCOLS = 16
COLS = 1568
GROUPS = COLS // GCOLS
EROWS = P * COLS
TAIL = EDGES - (P - 1) * COLS
FULL_GROUPS = TAIL // GCOLS
ITEM = 1024
IC = ITEM // P
ITEMS = (EDGES + BLOCKS * (ITEM - 1)) // ITEM + 1
PADDED = EROWS + ITEM
NO_NODE = 8192
BIG = 1e30
FD = DIM + HT
ACCW = DIM + HEADS

KC = DIM // P
HCH = -(-HID // P)
HLAST = HID - (HCH - 1) * P
HALF = HID // 2
W13 = 2 * HID
TILES = (2 * NODES + EXPERTS * (P - 1)) // P
SLOT_TILES = TILES + 2

IV = 5
UG = 2
LOOPS = ITEMS // IV
assert COLS % GCOLS == 0 and TAIL % GCOLS == 0 and EROWS >= EDGES
assert LOOPS * IV == ITEMS and LOOPS * UG == GROUPS and FULL_GROUPS % UG == 0
BC = 7
assert BLOCKS % BC == 0 and TILES % BC == 0


class Steps:

    def __init__(self, eng, sem):
        self.eng, self.sem, self.base, self.n = eng, sem, 0, 0

    def loop(self, i, per, first=0):
        assert self.per is None
        self.start, self.first, self.i, self.per, self.n = self.base, first, i, per, 0

    def end(self, rounds):
        assert self.n == self.per, (self.n, self.per)
        self.base, self.n, self.per = self.start + rounds * self.per, 0, None

    per = None

    def __call__(self, ins):
        ins.then_inc(self.sem, 1)
        self.n += 1
        if self.per is None:
            self.base += 1
            self.n = 0
            self.eng.wait_ge(self.sem, self.base)
        else:
            self.eng.wait_ge(self.sem, self.i * self.per + (self.start - self.first * self.per + self.n))


def wait_apart(eng, sem, value, tick):
    eng.wait_ge(sem, value)
    eng.sem_inc(tick, 1)


def flat(ap):
    return ap.rearrange("p a n -> p (a n)")


def join_stats(dve, step, stats, mv, tmp, var_ok):
    mean = [stats[:, :, 1], stats[:, :, 4]]
    dve.tensor_tensor(tmp[:, :, 0], mean[0], mean[1], ALU.subtract)
    dve.tensor_tensor(tmp[:, :, 1], stats[:, :, 2], stats[:, :, 5], ALU.add)
    step(dve.tensor_tensor(mv[:, :, 0], mean[0], mean[1], ALU.add))
    dve.tensor_scalar(mv[:, :, 0], mv[:, :, 0], 0.5, None, ALU.mult)
    step(dve.scalar_tensor_tensor(tmp[:, :, 0], tmp[:, :, 0], 0.25, tmp[:, :, 0], ALU.mult, ALU.mult))
    dve.scalar_tensor_tensor(mv[:, :, 1], tmp[:, :, 1], 1.0 / DIM, tmp[:, :, 0], ALU.mult, ALU.add).then_inc(var_ok, 1)
    dve.wait_ge(var_ok, 1)


def edge_slice(dram, lo, hi, col):
    width = dram.shape[1]
    return bass.AP(dram.tensor, col * width + lo * COLS * width, [(COLS * width, hi - lo), (width, GCOLS), (1, width)])


def edge_view(dram):
    return dram[0:EROWS, :].rearrange("(p t) d -> p t d", p=P)


def node_view(dram):
    return dram.rearrange("(b p) d -> p b d", p=P)


def gnn_moe_kernel(nc, x, src, dst, edge16, edge4, w_n, attn_l, attn_r, attn_m, router_w, w1, w2, w3, out):
    def dram(name, shape, dt=F32):
        return nc.dram_tensor(name, shape, dt, kind="Internal").ap()

    table = dram("table", (ROWS, FD))
    dst_pad = dram("dst_pad", (PADDED,), I32)
    src_pad = dram("src_pad", (EROWS,), I32)
    er_edges = dram("er_edges", (PADDED, HT))
    feat_edges = dram("feat_edges", (PADDED, DIM))
    p_edges = dram("p_edges", (PADDED, HEADS))
    w13_t = dram("w13_t", (EXPERTS, P, KC, W13))
    w2_t = dram("w2_t", (EXPERTS, P, HCH, DIM))
    x2_dram = dram("x2_dram", (ROWS, DIM))
    slots_x = dram("slots_x", (SLOT_TILES * P, DIM))
    slots_y = dram("slots_y", (SLOT_TILES * P, DIM))

    with ExitStack() as ctx:
        in_steps = []

        def sem(name, lasting=False):
            handle = nc.alloc_semaphore(name=name)
            if not lasting:
                in_steps.append(handle)
            return handle

        def clear_sems():
            nc.clear_and_free_semaphores(in_steps)
            in_steps.clear()
            nc.all_engine_barrier()

        def sb(stack, name, shape, dt=F32):
            return stack.enter_context(nc.sbuf_tensor(name, shape, dt))

        def ps(stack, name, shape):
            return stack.enter_context(nc.psum_tensor(name, shape, F32))

        dve_step, act_step, pool_step = (sem(n, lasting=True) for n in ("dve_step", "act_step", "pool_step"))
        dve_steps = Steps(nc.vector, dve_step)
        tick = sem("tick", lasting=True)

        ident = sb(ctx, "ident", [P, P])
        ones = sb(ctx, "ones", [P, P])
        iota_row = sb(ctx, "iota_row", [P, P])
        part = sb(ctx, "part", [P, 1])
        blk_i = sb(ctx, "blk_i", [1, ITEMS], I32)
        start_i = sb(ctx, "start_i", [1, ITEMS], I32)
        blk128 = sb(ctx, "blk128", [P, ITEMS])
        rt = sb(ctx, "rt", [P, KC, EXPERTS])
        lg = sb(ctx, "lg", [P, BLOCKS, EXPERTS])
        mv2 = sb(ctx, "mv2", [P, BLOCKS, 2])
        rstd2 = sb(ctx, "rstd2", [P, BLOCKS])
        zero_row = sb(ctx, "zero_row", [P, DIM])

        edges_ctx = ctx.enter_context(ExitStack())
        er = sb(edges_ctx, "er", [P, BLOCKS + 1, HT])
        dst_sb = sb(edges_ctx, "dst_sb", [P, COLS], I32)
        bm = sb(edges_ctx, "bm", [P, 8, HT])
        node_id = sb(edges_ctx, "node_id", [P, ITEMS])

        with ExitStack() as st:
            xall = sb(st, "xall", [P, BLOCKS, DIM])
            wall = sb(st, "wall", [P, KC, DIM + 2 * HT])
            wn_t = sb(st, "wn_t", [P, KC, DIM])
            bd = sb(st, "bd", [P, KC, 2, HT])
            zeros = sb(st, "zeros", [P, 2048])
            pad_i = sb(st, "pad_i", [64, 64], I32)
            rt_rows = sb(st, "rt_rows", [EXPERTS, DIM])
            stats = sb(st, "stats", [P, BLOCKS, 6])
            mv = sb(st, "mv", [P, BLOCKS, 2])
            tmp = sb(st, "tmp", [P, BLOCKS, 2])
            rstd = sb(st, "rstd", [P, BLOCKS])
            eps = sb(st, "eps", [P, 1])
            xt = sb(st, "xt", [P, 2, KC, P])
            xn = sb(st, "xn", [P, 2, DIM])
            fo = sb(st, "fo", [P, 2, FD])
            ps_w = ps(st, "ps_w", [P, 512])
            ps_t = [ps(st, f"ps_t{i}", [P, 512]) for i in range(2)]
            ps_f = [ps(st, f"ps_f{i}", [P, 512]) for i in range(2)]

            ident_zero, consts, zeroed, x_in, w_in = map(sem, ("ident_zero", "consts", "zeroed", "x_in", "w_in"))
            fills, pads, wt_ps, wt_sb, wlr_ps, wall_ok = map(sem, ("fills", "pads", "wt_ps", "wt_sb", "wlr_ps", "wall_ok"))
            stats_ok, var_ok, std_ok, xn_ok, xt_ps, xt_sb = map(sem, ("stats_ok", "var_ok", "std_ok", "xn_ok", "xt_ps", "xt_sb"))
            f_ps, f_sb = sem("f_ps"), sem("f_sb")
            f_out = [sem("f_out0"), sem("f_out1")]

            with nc.Block() as block:
                @block.gpsimd
                def _(pool):
                    pool.memset(ident[:, :], 0.0).then_inc(ident_zero, 1)
                    pool.memset(ones[:, :], 1.0).then_inc(consts, 1)
                    pool.iota(iota_row[:, :], pattern=[[1, P]], base=0, channel_multiplier=0,
                              allow_small_or_imprecise_dtypes=True).then_inc(consts, 1)
                    pool.iota(part[:, :], pattern=[[0, 1]], base=0, channel_multiplier=1,
                              allow_small_or_imprecise_dtypes=True).then_inc(consts, 1)
                    pool.wait_ge(ident_zero, 1)
                    pool.affine_select(out=ident[:, :], in_=ident[:, :], compare_op=ALU.not_equal, fill=1.0,
                                       base=0, pattern=[[-1, P]], channel_multiplier=1).then_inc(consts, 1)
                    pool.memset(zero_row[:, :], 0.0).then_inc(consts, 1)
                    pool.memset(zeros[:, :], 0.0).then_inc(zeroed, 1)
                    pool.memset(pad_i[:, 0:32], 0).then_inc(zeroed, 1)
                    pool.memset(pad_i[:, 32:64], NO_NODE).then_inc(zeroed, 1)

                @block.sync
                def _(sp):
                    xv = x[0:(BLOCKS - 1) * P, :].rearrange("(b p) d -> p b d", p=P)
                    sp.dma_start(xall[:, 0:BLOCKS - 1, :], xv).then_inc(x_in, 16)
                    sp.dma_start(wall[:, :, 0:DIM], w_n.rearrange("(k p) d -> p k d", p=P)).then_inc(w_in, 16)
                    sp.dma_start(rt_rows[:, :], router_w).then_inc(w_in, 16)
                    sp.wait_ge(dve_step, 4)
                    sp.dma_start(xall[0:LAST, BLOCKS - 1, :], x[(BLOCKS - 1) * P:NODES, :]).then_inc(x_in, 16)
                    for h in range(HEADS):
                        k, r = (h * HDIM) // P, (h * HDIM) % P
                        for s, a in enumerate((attn_l, attn_r)):
                            sp.dma_start(bd[r:r + HDIM, k, s, h * T:(h + 1) * T], a[h]).then_inc(w_in, 16)
                    for j in range(8):
                        sp.dma_start(bm[j * F:(j + 1) * F, j, :].rearrange("f (h t) -> f h t", h=HEADS),
                                     attn_m.rearrange("h f t -> f h t")).then_inc(w_in, 16)
                    with sp.Fori(0, BLOCKS - 1, 2) as b:
                        for u in range(2):
                            sp.wait_ge(f_sb, b + (u + 1))
                            sp.dma_start(table[ds((b + u) * P, P), :], fo[:, u, :]).then_inc(f_out[u], 16)
                    sp.wait_ge(f_sb, BLOCKS)
                    sp.dma_start(table[(BLOCKS - 1) * P:ROWS, :], fo[:, 0, :]).then_inc(f_out[0], 16)
                    sp.wait_ge(f_out[0], 16 * (BLOCKS // 2 + 1))
                    sp.wait_ge(f_out[1], 16 * (BLOCKS // 2))
                    sp.wait_ge(pads, 64)
                    sp.wait_ge(fills, 16 * 18)

                @block.scalar
                def _(act):
                    act.dma_start(dst_pad[0:EDGES].rearrange("(a n) -> a n", a=16),
                                  dst.rearrange("(a n) -> a n", a=16)).then_inc(pads, 16)
                    act.dma_start(src_pad[0:EDGES].rearrange("(a n) -> a n", a=16),
                                  src.rearrange("(a n) -> a n", a=16)).then_inc(pads, 16)
                    act.wait_ge(zeroed, 3)
                    n = (PADDED - EDGES) // 64
                    act.dma_start(dst_pad[EDGES:PADDED].rearrange("(a n) -> a n", n=n),
                                  pad_i[:, 32:32 + n]).then_inc(pads, 16)
                    n = (EROWS - EDGES) // 64
                    act.dma_start(src_pad[EDGES:EROWS].rearrange("(a n) -> a n", n=n),
                                  pad_i[:, 0:n]).then_inc(pads, 16)
                    act.dma_start(feat_edges[EROWS:PADDED, :].rearrange("(p j) d -> p (j d)", p=P),
                                  zeros[:, 0:IC * DIM]).then_inc(fills, 16)
                    act.dma_start(p_edges[EROWS:PADDED, :].rearrange("(p j) d -> p (j d)", p=P),
                                  zeros[:, 0:IC * HEADS]).then_inc(fills, 16)
                    sx = slots_x.rearrange("(p j) d -> p (j d)", p=P)
                    width = SLOT_TILES * DIM
                    for j in range(14):
                        lo, hi = min(j * 2048, width), min((j + 1) * 2048, width)
                        act.dma_start(sx[:, lo:hi], zeros[:, 0:hi - lo]).then_inc(fills, 16)
                    for j in range(2):
                        act.dma_start(slots_y[(TILES + j) * P:(TILES + j + 1) * P, :],
                                      zeros[:, 0:DIM]).then_inc(fills, 16)
                    act.wait_ge(wt_ps, 1)
                    act.copy(wn_t[:, 0, :], ps_w[:, 0:DIM])
                    act.copy(wn_t[:, 1, :], ps_w[:, DIM:2 * DIM]).then_inc(wt_sb, 1)
                    act.wait_ge(wlr_ps, 1)
                    for k in range(KC):
                        act.copy(wall[:, k, DIM:DIM + 2 * HT], ps_t[k][:, 0:2 * HT])
                    act.copy(rt[:, :, :], ps_f[0][:, 0:KC * EXPERTS].rearrange("p (k e) -> p k e", k=KC)).then_inc(wall_ok, 1)
                    act.wait_ge(var_ok, 1)
                    act.activation(rstd[:, :], mv[:, :, 1], ACT.Sqrt, bias=eps[:, 0:1]).then_inc(std_ok, 1)
                    with act.Fori(0, BLOCKS - 1, 2) as b:
                        for u in range(2):
                            act.wait_ge(xt_ps, b + (u + 1))
                            act.copy(xt[:, u, :, :], ps_t[u][:, 0:KC * P].rearrange("p (k n) -> p k n", k=KC)).then_inc(xt_sb, 1)
                    act.wait_ge(xt_ps, BLOCKS)
                    act.copy(xt[:, 0, :, :], ps_t[0][:, 0:KC * P].rearrange("p (k n) -> p k n", k=KC)).then_inc(xt_sb, 1)

                @block.vector
                def _(dve):
                    dve_steps(dve.memset(bd[:, :, :, :], 0.0))
                    dve_steps(dve.memset(bm[:, :, :], 0.0))
                    dve_steps(dve.memset(er[:, BLOCKS, :], 0.0))
                    dve_steps(dve.memset(xall[:, BLOCKS - 1, :], 0.0))
                    dve_steps(dve.memset(eps[:, :], LN_EPS))
                    dve.wait_ge(x_in, 32)
                    with dve.Fori(0, BLOCKS // BC) as c:
                        for j in range(BC):
                            dve.bn_stats(flat(stats[:, ds(c * BC + j, 1), :]), flat(xall[:, ds(c * BC + j, 1), :])).then_inc(stats_ok, 1)
                    dve.wait_ge(stats_ok, BLOCKS)
                    join_stats(dve, dve_steps, stats, mv, tmp, var_ok)
                    dve.wait_ge(std_ok, 1)
                    dve_steps(dve.reciprocal(rstd[:, :], rstd[:, :]))

                    def norm(b, u):
                        dve.tensor_scalar(xn[:, u, :], flat(xall[:, ds(b, 1), :]), mv[:, ds(b, 1), 0],
                                          rstd[:, ds(b, 1)], ALU.subtract, ALU.mult).then_inc(xn_ok, 1)

                    def rows_out(b, u):
                        dve.wait_ge(f_ps, b + 1)
                        dve.tensor_copy(fo[:, u, :], ps_f[u][:, 0:FD])
                        dve.tensor_copy(er[:, ds(b, 1), :], ps_f[u][:, FD:FD + HT].unsqueeze(1)).then_inc(f_sb, 1)

                    norm(0, 0)
                    norm(1, 1)
                    for u in range(2):
                        rows_out(u, u)
                        norm(2 + u, u)
                    with dve.Fori(2, BLOCKS - 3, 2) as b:
                        for u in range(2):
                            dve.wait_ge(f_out[u], b * 8)
                            rows_out(b + u, u)
                            norm(b + (2 + u), u)
                    for b in range(BLOCKS - 3, BLOCKS):
                        dve.wait_ge(f_out[b % 2], (b - b % 2) * 8)
                        rows_out(b, b % 2)
                        if b + 2 < BLOCKS:
                            norm(b + 2, b % 2)

                @block.tensor
                def _(pe):
                    pe.wait_ge(consts, 5)
                    pe.wait_ge(w_in, 16 * 26)
                    for k in range(KC):
                        for m in range(KC):
                            last = pe.transpose(ps_w[:, k * DIM + m * P:k * DIM + (m + 1) * P],
                                                wall[:, m, k * P:(k + 1) * P], ident[:, :])
                    last.then_inc(wt_ps, 1)
                    for k in range(KC):
                        pe.transpose(ps_f[0][:, k * EXPERTS:(k + 1) * EXPERTS], rt_rows[:, k * P:(k + 1) * P],
                                     ident[0:EXPERTS, 0:EXPERTS])
                    pe.wait_ge(wt_sb, 1)
                    for m in range(KC):
                        for k in range(KC):
                            last = pe.matmul(ps_t[m][:, 0:2 * HT], wn_t[:, k, m * P:(m + 1) * P],
                                             bd[:, k, :, :].rearrange("p s h -> p (s h)"), start=(k == 0), stop=(k == KC - 1))
                    last.then_inc(wlr_ps, 1)
                    pe.wait_ge(wall_ok, 1)

                    def turn(b, u):
                        pe.wait_ge(xn_ok, b + 1)
                        for k in range(KC):
                            last = pe.transpose(ps_t[u][:, k * P:(k + 1) * P],
                                                xn[:, u, k * P:(k + 1) * P], ident[:, :])
                        last.then_inc(xt_ps, 1)

                    def project(u):
                        for k in range(KC):
                            last = pe.matmul(ps_f[u][:, 0:DIM + 2 * HT], xt[:, u, k, :], wall[:, k, :],
                                             start=(k == 0), stop=(k == KC - 1))
                        last.then_inc(f_ps, 1)

                    turn(0, 0)
                    turn(1, 1)
                    for u in range(2):
                        pe.wait_ge(xt_sb, u + 1)
                        project(u)
                        turn(2 + u, u)
                    with pe.Fori(2, BLOCKS - 3, 2) as b:
                        for u in range(2):
                            pe.wait_ge(xt_sb, b + (u + 1))
                            pe.wait_ge(f_sb, b + (u - 1))
                            project(u)
                            turn(b + (2 + u), u)
                    for b in range(BLOCKS - 3, BLOCKS):
                        pe.wait_ge(xt_sb, b + 1)
                        pe.wait_ge(f_sb, b - 1)
                        project(b % 2)
                        if b + 2 < BLOCKS:
                            turn(b + 2, b % 2)

        with ExitStack() as st:
            junk = sb(st, "junk", [P, COLS])
            thr_i = sb(st, "thr_i", [P, BLOCKS], I32)
            thr = sb(st, "thr", [P, BLOCKS])
            cnt = sb(st, "cnt", [P, BLOCKS + 1])
            tri = sb(st, "tri", [P, BLOCKS])
            w_iota = sb(st, "w_iota", [P, ITEMS])
            se = sb(st, "se", [BLOCKS, 2])
            nblk = sb(st, "nblk", [BLOCKS, 1])
            nit_i = sb(st, "nit_i", [BLOCKS, 1], I32)
            nit = sb(st, "nit", [BLOCKS, 1])
            cend = sb(st, "cend", [BLOCKS, 1])
            dq = sb(st, "dq", [BLOCKS, 1])
            passed = sb(st, "passed", [BLOCKS, ITEMS])
            start_f = sb(st, "start_f", [1, ITEMS])
            wrow = [[sb(st, f"wrow{m}{i}", [P, HCH, DIM]) for i in range(2)] for m in range(2)]
            w2row = [sb(st, f"w2row{i}", [P, KC, HID]) for i in range(2)]
            w13o = [sb(st, f"w13o{i}", [P, KC, W13]) for i in range(2)]
            w2o = [sb(st, f"w2o{i}", [P, HCH, DIM]) for i in range(2)]
            ps_c = ps(st, "ps_c", [P, 512])
            ps_b = ps(st, "ps_b", [P, 512])
            ps_wt = [ps(st, f"ps_wt{i}", [P, 1024]) for i in range(2)]

            dst_in, b_const, thr_ok, cnt_ok, se_ps, nit_ok, cend_ps, passed_ok, list_ps = map(
                sem, ("dst_in", "b_const", "thr_ok", "cnt_ok", "se_ps", "nit_ok", "cend_ps", "passed_ok", "list_ps"))
            wrow_in = [sem("wrow_in0"), sem("wrow_in1")]
            w_out = [sem("w_out0"), sem("w_out1")]
            turned, turned_sb, out_free = sem("turned"), sem("turned_sb"), [sem("out_free0"), sem("out_free1")]
            TURNS = 2 * KC + HCH // 2

            def weight_turns(u):
                for m in range(2):
                    for k in range(KC):
                        yield [(c * P, P, wrow[m][u][0:(P if c < HCH - 1 else HLAST), c, k * P:(k + 1) * P]) for c in range(HCH)]
                for c2 in range(HCH // 2):
                    yield [((c % 2) * 512 + k * P, P if c < HCH - 1 else HLAST,
                            w2row[u][:, k, c * P:min((c + 1) * P, HID)]) for c in (2 * c2, 2 * c2 + 1) for k in range(KC)]

            with nc.Block() as block:
                @block.sync
                def _(sp):
                    sp.dma_start(dst_sb[:, :], dst_pad[0:EROWS].rearrange("(p t) -> p t", p=P)).then_inc(dst_in, 16)
                    full = (HCH - 1) * P
                    with sp.Fori(0, EXPERTS // 2) as i:
                        for u in range(2):
                            sp.wait_ge(turned, i * (2 * TURNS) + (u + 1) * TURNS)
                            e = i * 2 + u
                            for m, w in enumerate((w1, w3)):
                                sp.dma_start(wrow[m][u][:, 0:HCH - 1, :],
                                             w[ds(e, 1), 0:full, :].rearrange("a (c p) d -> p (a c) d", p=P)).then_inc(wrow_in[u], 16)
                                sp.dma_start(wrow[m][u][0:HLAST, HCH - 1, :],
                                             w[ds(e, 1), full:HID, :].rearrange("a p d -> (a p) d")).then_inc(wrow_in[u], 16)
                            sp.dma_start(w2row[u][:, :, :],
                                         w2[ds(e, 1), :, :].rearrange("a (k p) h -> p (a k) h", p=P)).then_inc(wrow_in[u], 16)

                @block.gpsimd
                def _(pool):
                    pool.memset(cnt[:, 0:1], 0.0).then_inc(b_const, 1)
                    pool.memset(tri[:, :], 1.0).then_inc(pool_step, 1)
                    pool.wait_ge(pool_step, 1)
                    pool.affine_select(out=tri[:, :], in_=tri[:, :], compare_op=ALU.is_ge, fill=0.0, base=0,
                                       pattern=[[1, BLOCKS]], channel_multiplier=-1).then_inc(b_const, 1)
                    pool.iota(w_iota[:, :], pattern=[[1, ITEMS]], base=0, channel_multiplier=0,
                              allow_small_or_imprecise_dtypes=True).then_inc(b_const, 1)
                    pool.iota(thr[:, :], pattern=[[P, BLOCKS]], base=P, channel_multiplier=0,
                              allow_small_or_imprecise_dtypes=True).then_inc(b_const, 1)
                    for u in range(2):
                        pool.memset(w2o[u][:, HCH - 1, :], 0.0).then_inc(out_free[u], 1)
                    with pool.Fori(0, EXPERTS // 2) as i:
                        for u in range(2):
                            e = i * 2 + u
                            pool.wait_ge(turned_sb, i * (2 * TURNS) + (u + 1) * TURNS + 2)
                            pool.dma_start(w13_t[ds(e, 1), :, :, :].rearrange("a p k n -> (a p) k n"), w13o[u][:, :, :]).then_inc(w_out[u], 16)
                            pool.dma_start(w2_t[ds(e, 1), :, :, :].rearrange("a p k n -> (a p) k n"), w2o[u][:, :, :]).then_inc(w_out[u], 16)
                            pool.wait_ge(w_out[u], i * 32 + 32)
                            pool.sem_inc(out_free[u], 1)

                @block.vector
                def _(dve):
                    dve.wait_ge(dst_in, 16)
                    dve.wait_ge(b_const, 4)
                    with dve.Fori(0, BLOCKS) as b:
                        dve.tensor_scalar(junk[:, :], dst_sb[:, :], thr[:, ds(b, 1)], 0.0, ALU.is_lt, ALU.add,
                                          accum_out=cnt[:, ds(b + 1, 1)]).then_inc(cnt_ok, 1)
                        dve.wait_ge(cnt_ok, b + 1)
                    dve.wait_ge(se_ps, 1)
                    dve_steps(dve.tensor_copy(se[:, :], ps_c[0:BLOCKS, 0:2]))
                    dve_steps(dve.tensor_tensor(nblk[:, :], se[:, 1:2], se[:, 0:1], ALU.subtract))
                    dve_steps(dve.tensor_scalar(nit_i[:, :], nblk[:, :], float(ITEM - 1), None, ALU.add))
                    shift = ITEM.bit_length() - 1
                    dve_steps(dve.tensor_scalar(nit_i[:, :], nit_i[:, :], shift, None, ALU.arith_shift_right))
                    dve_steps(dve.tensor_copy(nit[:, :], nit_i[:, :]))
                    dve.scalar_tensor_tensor(dq[:, :], nit[:, :], -float(ITEM), nblk[:, :], ALU.mult, ALU.add).then_inc(nit_ok, 1)
                    dve.wait_ge(cend_ps, 1)
                    dve_steps(dve.tensor_copy(cend[:, :], ps_c[0:BLOCKS, 8:9]))
                    dve.tensor_scalar(passed[:, :], w_iota[0:BLOCKS, :], cend[:, :], None, ALU.is_ge).then_inc(passed_ok, 1)
                    dve.wait_ge(list_ps, 1)
                    dve_steps(dve.tensor_copy(blk_i[:, :], ps_c[0:1, 16:16 + ITEMS]))
                    dve_steps(dve.tensor_scalar(blk128[:, :], ps_b[:, 0:ITEMS], float(P), None, ALU.mult))
                    dve_steps(dve.scalar_tensor_tensor(start_f[:, :], w_iota[0:1, :], float(ITEM), ps_b[0:1, 256:256 + ITEMS],
                                                       ALU.mult, ALU.add))
                    dve_steps(dve.tensor_scalar(start_i[:, :], start_f[:, :], float(EDGES), None, ALU.min))
                    dve_steps(dve.tensor_scalar(node_id[:, :], blk128[:, :], part[:, 0:1], None, ALU.add))

                @block.tensor
                def _(pe):
                    pe.sem_inc(turned, 2 * TURNS)
                    with pe.Fori(0, EXPERTS // 2) as i:
                        for u in range(2):
                            pe.wait_ge(wrow_in[u], i * 80 + 80)
                            for n, outs in enumerate(weight_turns(u)):
                                pe.wait_ge(turned_sb, i * (2 * TURNS) + (u * TURNS + n + 1))
                                tile = ps_wt[(u * TURNS + n) % 2]
                                for o, w, rows in outs:
                                    k = rows.shape[0]
                                    last = pe.transpose(tile[0:w, o:o + k], rows, ident[0:k, 0:k])
                                last.then_inc(turned, 1)
                    pe.wait_ge(cnt_ok, BLOCKS)
                    pe.matmul(ps_c[0:BLOCKS, 0:1], cnt[:, 0:BLOCKS], ones[:, 0:1], start=True, stop=True)
                    pe.matmul(ps_c[0:BLOCKS, 1:2], cnt[:, 1:BLOCKS + 1], ones[:, 0:1], start=True, stop=True).then_inc(se_ps, 1)
                    pe.wait_ge(nit_ok, 1)
                    pe.matmul(ps_c[0:BLOCKS, 8:9], tri[0:BLOCKS, :], nit[:, :], start=True, stop=True).then_inc(cend_ps, 1)
                    pe.wait_ge(passed_ok, 1)
                    pe.matmul(ps_c[0:1, 16:16 + ITEMS], ones[0:BLOCKS, 0:1], passed[:, :], start=True, stop=True)
                    pe.matmul(ps_b[:, 0:ITEMS], ones[0:BLOCKS, :], passed[:, :], start=True, stop=True)
                    pe.matmul(ps_b[0:1, 256:256 + ITEMS], dq[:, :], passed[:, :], start=True, stop=True).then_inc(list_ps, 1)

                @block.scalar
                def _(act):
                    act.sem_inc(turned_sb, 2)
                    with act.Fori(0, EXPERTS // 2) as i:
                        for u in range(2):
                            act.wait_ge(out_free[u], i + 1)
                            for n in range(TURNS):
                                act.wait_ge(turned, i * (2 * TURNS) + (2 * TURNS + u * TURNS + n + 1))
                                tile = ps_wt[(u * TURNS + n) % 2]
                                if n < 2 * KC:
                                    m, k = divmod(n, KC)
                                    last = act.copy(w13o[u][:, k, m * HID:(m + 1) * HID], tile[:, 0:HID])
                                else:
                                    c = 2 * (n - 2 * KC)
                                    if c + 1 < HCH - 1:
                                        last = act.copy(w2o[u][:, c:c + 2, :],
                                                        tile[:, :].rearrange("p (c d) -> p c d", c=2)[:, :, 0:DIM])
                                    else:
                                        act.copy(w2o[u][:, c, :], tile[:, 0:DIM])
                                        last = act.copy(w2o[u][0:HLAST, c + 1, :], tile[0:HLAST, 512:512 + DIM])
                                last.then_inc(turned_sb, 1)

        score_ctx = ctx.enter_context(ExitStack())
        left = sb(score_ctx, "left", [P, HEADS, COLS])
        late_ctx = ctx.enter_context(ExitStack())
        mask = sb(late_ctx, "mask", [P, COLS, T])
        with ExitStack() as st:
            src_sb = sb(st, "src_sb", [P, COLS], I32)
            idx = [sb(st, f"idx{u}", [P, GCOLS], I32) for u in range(UG)]
            rows = [sb(st, f"rows{u}", [P, GCOLS, FD]) for u in range(UG)]
            e16 = [sb(st, f"e16_{u}", [P, GCOLS, F]) for u in range(UG)]
            e16_t = sb(st, "e16_t", [P, UG, 2, P])
            term = [sb(st, f"term{u}", [P, GCOLS, HT]) for u in range(UG)]
            dst_row = [sb(st, f"dst_row{v}", [P, ITEM], I32) for v in range(IV)]
            hot_t = [sb(st, f"hot_t{v}", [P, ITEM]) for v in range(IV)]
            er_out = [sb(st, f"er_out{v}", [P, IC, HT]) for v in range(IV)]
            ps_er = [ps(st, f"ps_er{v}", [P, 512]) for v in range(IV)]
            ps_e16 = ps(st, "ps_e16", [P, 512])
            ps_em = [ps(st, f"ps_em{u}", [P, 512]) for u in range(UG)]

            def er_tile(v):
                return ps_er[v][:, 0:IC * HT]

            src_in, mask_zero, er_written, idx_ok = sem("src_in"), sem("mask_zero"), sem("er_written"), sem("idx_ok")
            e16_ps, e16_sb = sem("e16_ps"), sem("e16_sb")

            def sems(name, n):
                return [sem(f"{name}{k}") for k in range(n)]

            gathered, spilled, left_ok, e16_in, em_ok = (
                sems(n, UG) for n in ("gathered", "spilled", "left_ok", "e16_in", "em_ok"))
            dst_row_in, hot_ok, er_ps_ok, er_sb_ok, er_out_free = (
                sems(n, IV) for n in ("dst_row_in", "hot_ok", "er_ps_ok", "er_sb_ok", "er_out_free"))

            with nc.Block() as block:
                @block.gpsimd
                def _(pool):
                    pool.wait_ge(src_in, 16)
                    with pool.Fori(0, LOOPS) as i:
                        for u in range(UG):
                            pool.wait_ge(spilled[u], i * 16 + 16)
                            pool.wait_ge(left_ok[u], i + 1)
                            pool.tensor_copy(idx[u][:, :], src_sb[:, ds((i * UG + u) * GCOLS, GCOLS)]).then_inc(idx_ok, 1)
                            wait_apart(pool, idx_ok, i * UG + (u + 1), tick)
                            for t in range(GCOLS):
                                pool.indirect_dma_start(rows[u][:, t, :], None, table,
                                                        bass.IndirectOffsetOnAxis(ap=idx[u][:, t:t + 1], axis=0)).then_inc(gathered[u], 16)

                @block.sync
                def _(sp):
                    sp.dma_start(src_sb[:, :], src_pad.rearrange("(p t) -> p t", p=P)).then_inc(src_in, 16)
                    with sp.Fori(0, LOOPS) as i:
                        starts = []
                        for v in range(IV):
                            starts.append(sp.value_load(start_i[0:1, ds(i * IV + v, 1)], min_val=0, max_val=EDGES))
                            wait_apart(sp, hot_ok[v], i + 1, tick)
                            sp.dma_start(dst_row[v][:, :], dst_pad[ds(starts[v], ITEM)].partition_broadcast(P)).then_inc(dst_row_in[v], 16)
                        for v in range(IV):
                            wait_apart(sp, er_sb_ok[v], i + 2, tick)
                            sp.dma_start(er_edges[ds(starts[v], ITEM), :].rearrange("(p j) d -> p j d", p=P),
                                         er_out[v][:, :, :]).then_inc(er_written, 16)
                            sp.wait_ge(er_written, i * (16 * IV) + 16 * (v + 1))
                            sp.sem_inc(er_out_free[v], 1)

                @block.scalar
                def _(act):
                    for u in range(UG):
                        act.dma_start(feat_edges[EROWS + u * P:EROWS + (u + 1) * P, :], zero_row[:, :]).then_inc(spilled[u], 16)
                    for v in range(IV):
                        act.sem_inc(er_sb_ok[v], 1)
                        act.sem_inc(er_out_free[v], 1)
                    act.wait_ge(mask_zero, 1)

                    def body(i, cuts):
                        for u in range(UG):
                            g = i * UG + u
                            act.wait_ge(left_ok[u], i + 1)
                            for lo, hi in cuts:
                                for dst_ap, dram_ap in ((e16[u][lo:hi, :, :], edge16), (mask[lo:hi, ds(g * GCOLS, GCOLS), :], edge4)):
                                    act.dma_start(dst_ap, edge_slice(dram_ap, lo, hi, g * GCOLS)).then_inc(e16_in[u], 16)
                        act.wait_ge(e16_ps, i + 1)
                        act.copy(e16_t[:, :, :, :].rearrange("p u h n -> p (u h n)"), ps_e16[:, :]).then_inc(e16_sb, 1)
                        for v in range(IV):
                            act.wait_ge(er_ps_ok[v], i + 2)
                            act.wait_ge(er_out_free[v], i + 1)
                            act.copy(er_out[v][:, :, :], er_tile(v).rearrange("p (j d) -> p j d", j=IC)).then_inc(er_sb_ok[v], 1)
                        for u in range(UG):
                            act.wait_ge(gathered[u], i * (16 * GCOLS) + 16 * GCOLS)
                            act.dma_start(edge_view(feat_edges)[:, ds((i * UG + u) * GCOLS, GCOLS), :],
                                          rows[u][:, :, 0:DIM]).then_inc(spilled[u], 16)

                    with act.Fori(0, FULL_GROUPS // UG) as i:
                        body(i, ((0, 112), (112, P)))
                    with act.Fori(FULL_GROUPS // UG, LOOPS) as i:
                        body(i, ((0, 112), (112, P - 1)))
                    for u in range(UG):
                        act.wait_ge(spilled[u], LOOPS * 16 + 16)

                @block.vector
                def _(dve):
                    dve.memset(mask[:, :, :], 0.0).then_inc(mask_zero, 1)
                    for u in range(UG):
                        dve.sem_inc(left_ok[u], 1)
                    for v in range(IV):
                        dve.sem_inc(hot_ok[v], 1)
                    with dve.Fori(0, LOOPS) as i:
                        dve_steps.loop(i, 2 * UG)
                        for v in range(IV):
                            dve.wait_ge(dst_row_in[v], i * 16 + 16)
                            dve.wait_ge(er_ps_ok[v], i + 1)
                            dve.tensor_scalar(hot_t[v][:, :], dst_row[v][:, :], node_id[:, ds(i * IV + v, 1)], None,
                                              ALU.is_equal).then_inc(hot_ok[v], 1)
                        for u in range(UG):
                            g = i * UG + u
                            dve.wait_ge(left_ok[u], i + 1)
                            dve.wait_ge(em_ok[u], i + 1)
                            dve.wait_ge(gathered[u], i * (16 * GCOLS) + 16 * GCOLS)
                            dve_steps(dve.tensor_tensor(term[u][:, :, :], ps_em[u][:, :].rearrange("p (t d) -> p t d", t=GCOLS),
                                                        rows[u][:, :, DIM:FD], ALU.add))
                            masked = term[u][:, :, :].rearrange("p t (h k) -> p t h k", h=HEADS)
                            dve_steps(dve.tensor_tensor(masked, masked,
                                                        mask[:, ds(g * GCOLS, GCOLS), :].unsqueeze(2).to_broadcast([P, GCOLS, HEADS, T]),
                                                        ALU.mult))
                            dve.tensor_reduce(left[:, :, ds(g * GCOLS, GCOLS)].rearrange("p h t -> p t h"), masked,
                                              AX.X, ALU.add).then_inc(left_ok[u], 1)
                    dve_steps.end(LOOPS)

                @block.tensor
                def _(pe):
                    for v in range(IV):
                        pe.sem_inc(er_ps_ok[v], 1)
                    with pe.Fori(0, LOOPS) as i:
                        for u in range(UG):
                            pe.wait_ge(e16_in[u], i * 64 + 64)
                            pe.wait_ge(left_ok[u], i + 1)
                            for h in range(2):
                                last = pe.transpose(ps_e16[:, (u * 2 + h) * P:(u * 2 + h + 1) * P],
                                                    e16[u][:, h * 8:(h + 1) * 8, :].rearrange("p t f -> p (t f)"), ident[:, :])
                        last.then_inc(e16_ps, 1)
                        pe.wait_ge(e16_sb, i + 1)
                        for u in range(UG):
                            for h in range(2):
                                last = pe.matmul(ps_em[u][:, h * 256:(h + 1) * 256], e16_t[:, u, h, :],
                                                 bm[:, :, :].rearrange("p t d -> p (t d)"), start=True, stop=True)
                            last.then_inc(em_ok[u], 1)
                        for v in range(IV):
                            b = pe.value_load(blk_i[0:1, ds(i * IV + v, 1)], min_val=0, max_val=BLOCKS)
                            pe.wait_ge(hot_ok[v], i + 2)
                            pe.wait_ge(er_sb_ok[v], i + 1)
                            for j in range(IC):
                                last = pe.matmul(er_tile(v)[:, j * HT:(j + 1) * HT], hot_t[v][:, j::IC],
                                                 flat(er[:, ds(b, 1), :]), start=True, stop=True)
                            last.then_inc(er_ps_ok[v], 1)

        max_ctx = ctx.enter_context(ExitStack())
        top = sb(max_ctx, "top", [P, HEADS, COLS])
        same = sb(max_ctx, "same", [P, COLS + 1])
        first = sb(max_ctx, "first", [P, COLS])
        ends = sb(max_ctx, "ends", [P, 4, HEADS])
        CH = 98
        CHUNKS = COLS // CH
        with ExitStack() as st:
            er_in = [sb(st, f"er_in{u}", [P, CH, HT]) for u in range(2)]
            s_in, s_used = [sem("s_in0"), sem("s_in1")], sem("s_used")
            right = sb(st, "right", [P, HEADS, CH])
            cut = sb(st, "cut", [P, HEADS, CH])
            cmax = sb(st, "cmax", [P, CHUNKS, HEADS])
            dst_f = sb(st, "dst_f", [P, 2])

            with nc.Block() as block:
                @block.sync
                def _(sp):
                    with sp.Fori(0, CHUNKS // 2) as i:
                        for u in range(2):
                            sp.wait_ge(s_used, i * 2 + (u + 1))
                            sp.dma_start(er_in[u][:, :, :], edge_view(er_edges)[:, ds((i * 2 + u) * CH, CH), :]).then_inc(s_in[u], 16)

                @block.vector
                def _(dve):
                    dve.sem_inc(s_used, 2)
                    for j, col in enumerate((0, COLS - 1)):
                        dve_steps(dve.tensor_copy(dst_f[:, j:j + 1], dst_sb[:, col:col + 1]))
                    dve_steps(dve.tensor_tensor(same[:, 1:COLS], dst_sb[:, 1:COLS], dst_sb[:, 0:COLS - 1], ALU.is_equal))
                    dve_steps(dve.tensor_scalar(same[:, 1:COLS], same[:, 1:COLS], BIG, -BIG, ALU.mult, ALU.add))
                    dve_steps(dve.memset(same[:, 0:1], -BIG))
                    dve_steps(dve.memset(same[:, COLS:COLS + 1], 0.0))
                    dve_steps(dve.tensor_scalar(first[:, :], dst_sb[:, :], dst_f[:, 0:1], None, ALU.is_equal))
                    dve_steps(dve.tensor_scalar(first[:, :], first[:, :], BIG, -BIG, ALU.mult, ALU.add))
                    for j in range(2):
                        dve_steps(dve.tensor_copy(ends[:, 2 + j, :], dst_f[:, j:j + 1].to_broadcast([P, HEADS])))

                    def chunk(c, u, head_start):
                        cols = ds(c * CH, CH)
                        masked = er_in[u][:, :, :].rearrange("p t (h k) -> p t h k", h=HEADS)
                        dve_steps(dve.tensor_tensor(masked, masked, mask[:, cols, :].unsqueeze(2).to_broadcast([P, CH, HEADS, T]), ALU.mult))
                        dve_steps(dve.tensor_reduce(right[:, :, :].rearrange("p h t -> p t h"), masked, AX.X, ALU.add))
                        dve.sem_inc(s_used, 1)
                        e = left[:, :, cols]
                        dve_steps(dve.tensor_tensor(e, e, right[:, :, :], ALU.add))
                        dve_steps(dve.tensor_scalar(e, e, 1.0 / 3.0, None, ALU.mult))
                        dve_steps(dve.scalar_tensor_tensor(e, e, SLOPE, e, ALU.mult, ALU.max))
                        dve.tensor_tensor(cut[:, :, :], e, first[:, cols].unsqueeze(1).to_broadcast([P, HEADS, CH]), ALU.add)
                        for h in range(HEADS):
                            initial = 0.0 if head_start else top[:, h, ds(c * CH - 1, 1)]
                            last = dve.tensor_tensor_scan(top[:, h, cols], same[:, cols], left[:, h, cols], initial, ALU.add, ALU.max)
                        dve_steps(last)
                        dve_steps(dve.tensor_reduce(cmax[:, ds(c, 1), :].rearrange("p c h -> p (c h)"), cut[:, :, :], AX.X, ALU.max))

                    PER = 7
                    for c in range(2):
                        dve.wait_ge(s_in[c], 16)
                        chunk(c, c, c == 0)
                    with dve.Fori(1, CHUNKS // 2) as i:
                        dve_steps.loop(i, 2 * PER, 1)
                        for u in range(2):
                            dve.wait_ge(s_in[u], i * 16 + 16)
                            chunk(i * 2 + u, u, False)
                    dve_steps.end(CHUNKS // 2 - 1)
                    dve_steps(dve.tensor_copy(ends[:, 0, :], top[:, :, COLS - 1]))
                    dve_steps(dve.tensor_reduce(ends[:, 1, :], cmax[:, :, :].rearrange("p c h -> p h c"), AX.X, ALU.max))

        with ExitStack() as st:
            rowf = sb(st, "rowf", [HEADS, 4, P])
            cont = sb(st, "cont", [HEADS, P + 1])
            sing = sb(st, "sing", [HEADS, P])
            pen = sb(st, "pen", [HEADS, 2, P])
            run = sb(st, "run", [HEADS, 2, P])
            cf = sb(st, "cf", [HEADS, P])
            cb = sb(st, "cb", [HEADS, P])
            outer = sb(st, "outer", [HEADS, 2, P])
            beyond = sb(st, "beyond", [P, 2, HEADS])
            late_p = sb(st, "late_p", [P, COLS // 2, HEADS])
            p_out = [mask[:, :, :].rearrange("p (t a) k -> p t (a k)", a=2), late_p[:, :, :]]
            ps_x = ps(st, "ps_x", [P, 512])
            ps_y = ps(st, "ps_y", [P, 512])
            ends_ps, outer_ok, outer_ps, less_max, exp_ok, p_written = map(
                sem, ("ends_ps", "outer_ok", "outer_ps", "less_max", "exp_ok", "p_written"))

            with nc.Block() as block:
                @block.tensor
                def _(pe):
                    for j in range(4):
                        last = pe.transpose(ps_x[0:HEADS, j * P:(j + 1) * P], ends[:, j, :], ident[:, :])
                    last.then_inc(ends_ps, 1)
                    pe.wait_ge(outer_ok, 1)
                    for j in range(2):
                        last = pe.transpose(ps_y[:, j * HEADS:(j + 1) * HEADS], outer[:, j, :], ident[0:HEADS, 0:HEADS])
                    last.then_inc(outer_ps, 1)

                @block.vector
                def _(dve):
                    step = dve_steps
                    dve.wait_ge(ends_ps, 1)
                    step(dve.tensor_copy(rowf[:, :, :], ps_x[0:HEADS, :].rearrange("h (j p) -> h j p", j=4)))
                    m_last, m_first, d_first, d_last = (rowf[:, j, :] for j in range(4))
                    step(dve.memset(cont[:, :], 0.0))
                    step(dve.tensor_tensor(cont[:, 1:P], rowf[:, 2, 1:P], rowf[:, 3, 0:P - 1], ALU.is_equal))
                    step(dve.tensor_scalar(cont[:, :], cont[:, :], BIG, -BIG, ALU.mult, ALU.add))
                    step(dve.tensor_tensor(sing[:, :], d_first, d_last, ALU.is_equal))
                    step(dve.tensor_scalar(sing[:, :], sing[:, :], BIG, -BIG, ALU.mult, ALU.add))
                    step(dve.tensor_tensor(pen[:, 0, :], sing[:, :], cont[:, 0:P], ALU.add))
                    step(dve.tensor_tensor(pen[:, 1, :], sing[:, :], cont[:, 1:P + 1], ALU.add))
                    step(dve.tensor_tensor_scan(run[:, 0, :], pen[:, 0, :], m_last, -BIG, ALU.add, ALU.max))
                    step(dve.tensor_tensor_scan(run[:, 1, ::-1], pen[:, 1, ::-1], rowf[:, 1, ::-1], -BIG, ALU.add, ALU.max))
                    step(dve.memset(cf[:, :], -BIG))
                    step(dve.memset(cb[:, :], -BIG))
                    step(dve.tensor_tensor(cf[:, 1:P], run[:, 0, 0:P - 1], cont[:, 1:P], ALU.add))
                    step(dve.tensor_tensor(cb[:, 0:P - 1], run[:, 1, 1:P], cont[:, 1:P], ALU.add))
                    step(dve.tensor_tensor(outer[:, 0, :], cf[:, :], sing[:, :], ALU.add))
                    step(dve.tensor_tensor(outer[:, 1, :], cb[:, :], sing[:, :], ALU.add))
                    step(dve.tensor_tensor(outer[:, 0, :], outer[:, 0, :], cb[:, :], ALU.max))
                    dve.tensor_tensor(outer[:, 1, :], outer[:, 1, :], cf[:, :], ALU.max).then_inc(outer_ok, 1)
                    dve.wait_ge(outer_ps, 1)
                    step(dve.tensor_copy(beyond[:, :, :], ps_y[:, 0:2 * HEADS].rearrange("p (j h) -> p j h", j=2)))
                    for h in range(HEADS):
                        step(dve.tensor_tensor_scan(top[:, h, ::-1], same[:, 1:COLS + 1][:, ::-1], top[:, h, ::-1],
                                                    beyond[:, 0, h:h + 1], ALU.add, ALU.max))
                        step(dve.scalar_tensor_tensor(top[:, h, :], first[:, :], beyond[:, 1, h:h + 1], top[:, h, :],
                                                      ALU.add, ALU.max))
                        dve.tensor_tensor(left[:, h, :], left[:, h, :], top[:, h, :], ALU.subtract).then_inc(less_max, 1)

                @block.scalar
                def _(act):
                    for h in range(HEADS):
                        act.wait_ge(less_max, h + 1)
                        for j in range(2):
                            n = COLS // 2
                            act.activation(p_out[j][:, :, h], left[:, h, j * n:(j + 1) * n], ACT.Exp).then_inc(exp_ok, 1)

                @block.sync
                def _(sp):
                    sp.wait_ge(exp_ok, 2 * HEADS)
                    for j in range(2):
                        n = COLS // 2
                        sp.dma_start(edge_view(p_edges)[:, j * n:(j + 1) * n, :], p_out[j]).then_inc(p_written, 16)
                    sp.wait_ge(p_written, 32)
        max_ctx.close()
        late_ctx.close()
        score_ctx.close()
        edges_ctx.close()

        x2_ctx = ctx.enter_context(ExitStack())
        xall = sb(x2_ctx, "xall2", [P, BLOCKS, DIM])
        acc_ctx = ctx.enter_context(ExitStack())
        acc = sb(acc_ctx, "acc", [P, BLOCKS + 1, ACCW])
        x_in2, x_zero = sem("x_in2"), sem("x_zero")
        with ExitStack() as st:
            msg = [sb(st, f"msg{v}", [P, IC, ACCW]) for v in range(IV)]
            hot = [sb(st, f"hot{v}", [P, IC, P]) for v in range(IV)]
            dst_it = [sb(st, f"dst_it{v}", [P, IC], I32) for v in range(IV)]
            dst_rel = [sb(st, f"dst_rel{v}", [P, IC]) for v in range(IV)]
            ps_acc = [ps(st, f"ps_acc{v}", [P, 512]) for v in range(IV)]
            item_in, rel_ok, hot_made, msg_ok, sum_ok, acc_ok = (
                [sem(f"{n}{v}") for v in range(IV)] for n in ("item_in", "rel_ok", "hot_made", "msg_ok", "sum_ok", "acc_ok"))
            acc_zero = sem("acc_zero")
            pool_msg = [sem(f"pool_msg{v}") for v in range(IV)]
            POOL_FROM = IC - 2

            def weigh(eng, v, lo, hi):
                rows4 = msg[v][:, lo:hi, 0:DIM].rearrange("p j (h d) -> p j h d", h=HEADS)
                p4 = msg[v][:, lo:hi, DIM:ACCW].unsqueeze(3).to_broadcast([P, hi - lo, HEADS, HDIM])
                return eng.tensor_tensor(rows4, rows4, p4, ALU.mult)

            with nc.Block() as block:
                @block.sync
                def _(sp):
                    sp.wait_ge(x_zero, 1)
                    sp.dma_start(xall[:, 0:BLOCKS - 1, :], x[0:(BLOCKS - 1) * P, :].rearrange("(b p) d -> p b d", p=P)).then_inc(x_in2, 16)
                    sp.dma_start(xall[0:LAST, BLOCKS - 1, :], x[(BLOCKS - 1) * P:NODES, :]).then_inc(x_in2, 16)
                    with sp.Fori(0, LOOPS) as i:
                        for v in range(IV):
                            k0 = sp.value_load(start_i[0:1, ds(i * IV + v, 1)], min_val=0, max_val=EDGES)
                            wait_apart(sp, sum_ok[v], i + 1, tick)
                            sp.dma_start(msg[v][:, :, 0:DIM], feat_edges[ds(k0, ITEM), :].rearrange("(p j) d -> p j d", p=P)).then_inc(item_in[v], 16)
                            sp.dma_start(msg[v][:, :, DIM:ACCW], p_edges[ds(k0, ITEM), :].rearrange("(p j) d -> p j d", p=P)).then_inc(item_in[v], 16)
                            sp.dma_start(dst_it[v][:, :], dst_pad[ds(k0, ITEM)].rearrange("(p j) -> p j", p=P)).then_inc(item_in[v], 16)

                @block.gpsimd
                def _(pool):
                    pool.memset(xall[:, BLOCKS - 1, :], 0.0).then_inc(x_zero, 1)
                    with pool.Fori(0, LOOPS) as i:
                        for v in range(IV):
                            pool.wait_ge(item_in[v], i * 48 + 48)
                            weigh(pool, v, POOL_FROM, IC).then_inc(pool_msg[v], 1)

                @block.vector
                def _(dve):
                    dve.memset(acc[:, :, :], 0.0).then_inc(acc_zero, 1)
                    for v in range(IV):
                        dve.sem_inc(acc_ok[v], 1)
                    dve.wait_ge(acc_zero, 1)

                    def make(i, v):
                        dve.wait_ge(item_in[v], i * 48 + 48)
                        dve.tensor_scalar(dst_rel[v][:, :], dst_it[v][:, :], blk128[:, ds(i * IV + v, 1)], None,
                                          ALU.subtract).then_inc(rel_ok[v], 1)
                        weigh(dve, v, 0, POOL_FROM).then_inc(msg_ok[v], 1)
                        dve.wait_ge(rel_ok[v], i + 1)
                        dve.tensor_tensor(hot[v][:, :, :], iota_row[:, :].unsqueeze(1).to_broadcast([P, IC, P]),
                                          dst_rel[v][:, :].unsqueeze(2).to_broadcast([P, IC, P]), ALU.is_equal).then_inc(hot_made[v], 1)

                    def add(i, v):
                        b = dve.value_load(blk_i[0:1, ds(i * IV + v, 1)], min_val=0, max_val=BLOCKS)
                        dve.wait_ge(sum_ok[v], i + 2)
                        if v:
                            dve.wait_ge(acc_ok[v - 1], i + 2)
                        else:
                            dve.wait_ge(acc_ok[IV - 1], i + 1)
                        dve.tensor_tensor(flat(acc[:, ds(b, 1), :]), flat(acc[:, ds(b, 1), :]), ps_acc[v][:, 0:ACCW],
                                          ALU.add).then_inc(acc_ok[v], 1)

                    LAG = 2
                    for v in range(IV):
                        make(0, v)
                        if v >= LAG:
                            add(0, v - LAG)
                    with dve.Fori(1, LOOPS) as i:
                        for v in range(IV):
                            make(i, v)
                            if v >= LAG:
                                add(i, v - LAG)
                            else:
                                add(i - 1, v - LAG + IV)
                    for v in range(IV - LAG, IV):
                        add(LOOPS - 1, v)
                    dve.wait_ge(acc_ok[IV - 1], LOOPS + 1)
                    dve.wait_ge(x_in2, 32)

                @block.tensor
                def _(pe):
                    for v in range(IV):
                        pe.sem_inc(sum_ok[v], 1)
                    with pe.Fori(0, LOOPS) as i:
                        for v in range(IV):
                            pe.wait_ge(hot_made[v], i + 1)
                            pe.wait_ge(msg_ok[v], i + 1)
                            pe.wait_ge(pool_msg[v], i + 1)
                            pe.wait_ge(acc_ok[v], i + 1)
                            for j in range(IC):
                                last = pe.matmul(ps_acc[v][:, 0:ACCW], hot[v][:, j, :], msg[v][:, j, :],
                                                 start=(j == 0), stop=(j == IC - 1))
                            last.then_inc(sum_ok[v], 1)

        with ExitStack() as st:
            inv = sb(st, "inv", [P, BLOCKS, HEADS])
            stats = sb(st, "stats2", [P, BLOCKS, 6])
            tmp = sb(st, "tmp2", [P, BLOCKS, 2])
            eps = sb(st, "eps2", [P, 1])
            xn = sb(st, "xn2", [P, 2, DIM])
            xt = sb(st, "xt2", [P, 2, KC, P])
            ps_t = [ps(st, f"ps_t2{i}", [P, 512]) for i in range(2)]
            ps_l = [ps(st, f"ps_l{i}", [P, 512]) for i in range(2)]
            x2_ok, stats_ok, var_ok, std_ok, xn_ok, xt_ps, xt_sb, l_ps, l_sb, x2_out = map(
                sem, ("x2_ok", "stats2_ok", "var2_ok", "std2_ok", "xn2_ok", "xt2_ps", "xt2_sb", "l_ps", "l_sb", "x2_out"))

            with nc.Block() as block:
                @block.vector
                def _(dve):
                    step = dve_steps
                    step(dve.memset(eps[:, :], LN_EPS))
                    step(dve.tensor_scalar(inv[:, :, :], acc[:, 0:BLOCKS, DIM:ACCW], 0.5, None, ALU.max))
                    step(dve.reciprocal(inv[:, :, :], inv[:, :, :]))
                    with dve.Fori(0, BLOCKS // BC) as c:
                        step.loop(c, 2)
                        cb = ds(c * BC, BC)
                        rows4 = acc[:, cb, 0:DIM].rearrange("p b (h d) -> p b h d", h=HEADS)
                        step(dve.tensor_tensor(rows4, rows4, inv[:, cb, :].unsqueeze(3).to_broadcast([P, BC, HEADS, HDIM]), ALU.mult))
                        step(dve.tensor_tensor(xall[:, cb, :], xall[:, cb, :], acc[:, cb, 0:DIM], ALU.add))
                        for j in range(BC):
                            dve.bn_stats(flat(stats[:, ds(c * BC + j, 1), :]), flat(xall[:, ds(c * BC + j, 1), :])).then_inc(stats_ok, 1)
                    step.end(BLOCKS // BC)
                    dve.wait_ge(stats_ok, BLOCKS)
                    join_stats(dve, step, stats, mv2, tmp, var_ok)
                    dve.wait_ge(std_ok, 1)
                    step(dve.reciprocal(rstd2[:, :], rstd2[:, :]))

                    def norm(b, u):
                        dve.tensor_scalar(xn[:, u, :], flat(xall[:, ds(b, 1), :]), mv2[:, ds(b, 1), 0],
                                          rstd2[:, ds(b, 1)], ALU.subtract, ALU.mult).then_inc(xn_ok, 1)

                    norm(0, 0)
                    norm(1, 1)
                    for u in range(2):
                        dve.wait_ge(xt_ps, u + 1)
                        norm(2 + u, u)
                    with dve.Fori(2, BLOCKS - 3, 2) as b:
                        for u in range(2):
                            dve.wait_ge(xt_ps, b + (u + 1))
                            norm(b + (2 + u), u)
                    dve.wait_ge(xt_ps, BLOCKS - 2)
                    norm(BLOCKS - 1, (BLOCKS - 1) % 2)

                @block.sync
                def _(sp):
                    sp.wait_ge(stats_ok, BLOCKS)
                    sp.dma_start(node_view(x2_dram), xall[:, :, :]).then_inc(x2_out, 16)
                    sp.wait_ge(x2_out, 16)

                @block.scalar
                def _(act):
                    act.wait_ge(var_ok, 1)
                    act.activation(rstd2[:, :], mv2[:, :, 1], ACT.Sqrt, bias=eps[:, 0:1]).then_inc(std_ok, 1)

                    def copy_xt(b, u):
                        act.wait_ge(xt_ps, b + 1)
                        act.copy(xt[:, u, :, :], ps_t[u][:, 0:KC * P].rearrange("p (k n) -> p k n", k=KC)).then_inc(xt_sb, 1)

                    def copy_logits(b, u):
                        act.wait_ge(l_ps, b + 1)
                        act.copy(flat(lg[:, ds(b, 1), :]), ps_l[u][:, 0:EXPERTS]).then_inc(l_sb, 1)

                    copy_xt(0, 0)
                    copy_xt(1, 1)
                    with act.Fori(0, BLOCKS - 3, 2) as b:
                        for u in range(2):
                            copy_logits(b + u, u)
                            copy_xt(b + (2 + u), u)
                    copy_logits(BLOCKS - 3, 0)
                    copy_xt(BLOCKS - 1, 0)
                    copy_logits(BLOCKS - 2, 1)
                    copy_logits(BLOCKS - 1, 0)

                @block.tensor
                def _(pe):
                    def turn(b, u):
                        pe.wait_ge(xn_ok, b + 1)
                        for k in range(KC):
                            last = pe.transpose(ps_t[u][:, k * P:(k + 1) * P], xn[:, u, k * P:(k + 1) * P], ident[:, :])
                        last.then_inc(xt_ps, 1)

                    def logits(b, u):
                        pe.wait_ge(xt_sb, b + 1)
                        for k in range(KC):
                            last = pe.matmul(ps_l[u][:, 0:EXPERTS], xt[:, u, k, :], rt[:, k, :], start=(k == 0), stop=(k == KC - 1))
                        last.then_inc(l_ps, 1)

                    turn(0, 0)
                    turn(1, 1)
                    for b in range(2):
                        logits(b, b)
                        turn(2 + b, b)
                    with pe.Fori(2, BLOCKS - 3, 2) as b:
                        for u in range(2):
                            pe.wait_ge(l_sb, b + (u - 1))
                            logits(b + u, u)
                            turn(b + (2 + u), u)
                    for b in range(BLOCKS - 3, BLOCKS):
                        pe.wait_ge(l_sb, b - 1)
                        logits(b, b % 2)
                        if b + 2 < BLOCKS:
                            turn(b + 2, b % 2)
        acc_ctx.close()
        clear_sems()

        w13 = sb(ctx, "w13", [P, EXPERTS, KC * W13])
        route_ctx = ctx.enter_context(ExitStack())
        gates = sb(route_ctx, "gates", [P, 2, BLOCKS])
        slots = sb(route_ctx, "slots", [P, 2, BLOCKS], I32)
        tile_expert = sb(route_ctx, "tile_expert", [1, TILES], I32)
        weights_in = sem("weights_in")
        with ExitStack() as st:
            wide = [P, BLOCKS, EXPERTS]
            prob, hit, pick1, pick2, slot = (sb(st, n, wide) for n in ("prob", "hit", "pick1", "pick2", "slot"))
            total, seen, before = (sb(st, n, [P, EXPERTS, BLOCKS]) for n in ("total", "seen", "before"))
            best = sb(st, "best", [P, 3, BLOCKS])
            den = sb(st, "den", [P, BLOCKS])
            rank = sb(st, "rank", [P, EXPERTS])
            real = sb(st, "real", [P, BLOCKS])
            spare = sb(st, "spare", [P, 2, BLOCKS])
            slots_f = sb(st, "slots_f", [P, 2, BLOCKS])
            upper = sb(st, "upper", [P, P])
            tiles_i = sb(st, "tiles_i", [P, EXPERTS], I32)
            tiles = sb(st, "tiles", [P, EXPERTS])
            tend = sb(st, "tend", [P, EXPERTS])
            tbase = sb(st, "tbase", [P, EXPERTS])
            tau = sb(st, "tau", [1, TILES])
            past = sb(st, "past", [1, TILES, EXPERTS])
            texp = sb(st, "texp", [1, TILES])
            row = [sb(st, f"row{j}", [P, DIM]) for j in range(BC)]
            row_slot = [sb(st, f"row_slot{j}", [P, 2], I32) for j in range(BC)]
            ps_before = ps(st, "ps_before", [P, 512])
            ps_total = ps(st, "ps_total", [P, 512])
            r_const, less_ok, exp_done, pick_ok, rank_ps = map(sem, ("r_const", "less_ok", "exp_done", "pick_ok", "rank_ps"))
            row_ok = sem("row_ok")
            sent = [sem(f"sent{j}") for j in range(BC)]

            def over(ap):
                return ap.unsqueeze(2).to_broadcast(wide)

            with nc.Block() as block:
                @block.gpsimd
                def _(pool):
                    pool.iota(rank[:, :], pattern=[[-1, EXPERTS]], base=EXPERTS, channel_multiplier=0,
                              allow_small_or_imprecise_dtypes=True).then_inc(r_const, 1)
                    pool.iota(real[:, :], pattern=[[P, BLOCKS]], base=0, channel_multiplier=1,
                              allow_small_or_imprecise_dtypes=True).then_inc(r_const, 1)
                    pool.iota(tau[:, :], pattern=[[1, TILES]], base=0, channel_multiplier=0,
                              allow_small_or_imprecise_dtypes=True).then_inc(r_const, 1)
                    pool.memset(upper[:, :], 1.0).then_inc(pool_step, 1)
                    pool.wait_ge(pool_step, 2)
                    pool.affine_select(out=upper[:, :], in_=upper[:, :], compare_op=ALU.is_ge, fill=0.0, base=-1,
                                       pattern=[[1, P]], channel_multiplier=-1).then_inc(r_const, 1)

                    with pool.Fori(0, BLOCKS // BC) as c:
                        for j in range(BC):
                            wait_apart(pool, row_ok, c * BC + (j + 1), tick)
                            for k in range(2):
                                pool.indirect_dma_start(slots_x, bass.IndirectOffsetOnAxis(ap=row_slot[j][:, k:k + 1], axis=0),
                                                        row[j][:, :], None).then_inc(sent[j], 16)
                    for j in range(BC):
                        pool.wait_ge(sent[j], 32 * (BLOCKS // BC))

                @block.sync
                def _(sp):
                    for e in range(EXPERTS):
                        sp.dma_start(w13[:, e, :], w13_t[e].rearrange("p k n -> p (k n)")).then_inc(weights_in, 16)
                    sp.wait_ge(weights_in, 16 * EXPERTS)

                @block.scalar
                def _(act):
                    act.wait_ge(less_ok, 1)
                    act.activation(prob[:, :, :], prob[:, :, :], ACT.Exp).then_inc(exp_done, 1)

                @block.tensor
                def _(pe):
                    pe.wait_ge(pick_ok, 1)
                    chosen = hit[:, :, :].rearrange("p b e -> p (b e)")
                    pe.matmul(ps_before[:, 0:BLOCKS * EXPERTS], upper[:, :], chosen, start=True, stop=True)
                    pe.matmul(ps_total[:, 0:BLOCKS * EXPERTS], ones[:, :], chosen, start=True, stop=True).then_inc(rank_ps, 1)

                @block.vector
                def _(dve):
                    step = dve_steps
                    dve.wait_ge(r_const, 4)
                    step(dve.tensor_reduce(den[:, :], lg[:, :, :], AX.X, ALU.max))
                    dve.tensor_tensor(prob[:, :, :], lg[:, :, :], over(den[:, :]), ALU.subtract).then_inc(less_ok, 1)
                    dve.wait_ge(exp_done, 1)
                    step(dve.tensor_reduce(den[:, :], prob[:, :, :], AX.X, ALU.add))
                    step(dve.reciprocal(den[:, :], den[:, :]))
                    step(dve.tensor_tensor(prob[:, :, :], prob[:, :, :], over(den[:, :]), ALU.mult))

                    def pick(n, out):
                        step(dve.tensor_reduce(best[:, n, :], prob[:, :, :], AX.X, ALU.max))
                        step(dve.tensor_tensor(hit[:, :, :], prob[:, :, :], over(best[:, n, :]), ALU.is_equal))
                        step(dve.tensor_tensor(hit[:, :, :], hit[:, :, :], rank[:, :].unsqueeze(1).to_broadcast(wide), ALU.mult))
                        step(dve.tensor_reduce(best[:, 2, :], hit[:, :, :], AX.X, ALU.max))
                        step(dve.tensor_tensor(out[:, :, :], hit[:, :, :], over(best[:, 2, :]), ALU.is_equal))

                    pick(0, pick1)
                    step(dve.scalar_tensor_tensor(prob[:, :, :], pick1[:, :, :], -2.0, prob[:, :, :], ALU.mult, ALU.add))
                    pick(1, pick2)
                    step(dve.scalar_tensor_tensor(den[:, :], best[:, 0, :], 1e-9, best[:, 1, :], ALU.add, ALU.add))
                    step(dve.reciprocal(den[:, :], den[:, :]))
                    for n in range(2):
                        step(dve.tensor_tensor(gates[:, n, :], best[:, n, :], den[:, :], ALU.mult))
                    step(dve.tensor_scalar(real[:, :], real[:, :], float(NODES), None, ALU.is_lt))
                    for n in range(2):
                        step(dve.tensor_scalar(spare[:, n, :], real[:, :], -1.0, 1.0, ALU.mult, ALU.add))
                        step(dve.tensor_scalar(den[:, 0:1], part[:, :], float((TILES + n) * P), None, ALU.add))
                        step(dve.tensor_scalar(spare[:, n, :], spare[:, n, :], den[:, 0:1], None, ALU.mult))
                    step(dve.tensor_tensor(hit[:, :, :], pick1[:, :, :], pick2[:, :, :], ALU.add))
                    dve.tensor_tensor(hit[:, :, :], hit[:, :, :], over(real[:, :]), ALU.mult).then_inc(pick_ok, 1)
                    dve.wait_ge(rank_ps, 1)
                    step(dve.tensor_copy(total[:, :, :], ps_total[:, 0:BLOCKS * EXPERTS].rearrange("p (b e) -> p e b", e=EXPERTS)))
                    step(dve.memset(before[:, :, :], 1.0))
                    for e in range(EXPERTS):
                        step(dve.tensor_tensor_scan(seen[:, e, :], before[:, e, :], total[:, e, :], 0.0, ALU.mult, ALU.add))
                    step(dve.tensor_tensor(before[:, :, :], seen[:, :, :], total[:, :, :], ALU.subtract))
                    step(dve.tensor_scalar(tiles_i[:, :], seen[:, :, BLOCKS - 1], float(P - 1), None, ALU.add))
                    step(dve.tensor_scalar(tiles_i[:, :], tiles_i[:, :], P.bit_length() - 1, None, ALU.arith_shift_right))
                    step(dve.tensor_copy(tiles[:, :], tiles_i[:, :]))
                    step(dve.memset(tbase[:, :], 1.0))
                    step(dve.tensor_tensor_scan(tend[:, :], tbase[:, :], tiles[:, :], 0.0, ALU.mult, ALU.add))
                    step(dve.tensor_tensor(tbase[:, :], tend[:, :], tiles[:, :], ALU.subtract))
                    step(dve.scalar_tensor_tensor(slot[:, :, :], tbase[:, :].unsqueeze(1).to_broadcast(wide), float(P),
                                                  ps_before[:, 0:BLOCKS * EXPERTS].rearrange("p (b e) -> p b e", e=EXPERTS),
                                                  ALU.mult, ALU.add))
                    step(dve.tensor_tensor(slot[:, :, :], slot[:, :, :], before[:, :, :].rearrange("p e b -> p b e"), ALU.add))
                    for n, choice in enumerate((pick1, pick2)):
                        step(dve.tensor_tensor(choice[:, :, :], choice[:, :, :], slot[:, :, :], ALU.mult))
                        step(dve.tensor_reduce(slots_f[:, n, :], choice[:, :, :], AX.X, ALU.add))
                        step(dve.tensor_tensor(slots_f[:, n, :], slots_f[:, n, :], real[:, :], ALU.mult))
                        step(dve.tensor_tensor(slots_f[:, n, :], slots_f[:, n, :], spare[:, n, :], ALU.add))
                    step(dve.tensor_copy(slots[:, :, :], slots_f[:, :, :]))
                    step(dve.tensor_tensor(past[:, :, :], tau[:, :].unsqueeze(2).to_broadcast([1, TILES, EXPERTS]),
                                           tend[0:1, :].unsqueeze(1).to_broadcast([1, TILES, EXPERTS]), ALU.is_ge))
                    step(dve.tensor_reduce(texp[:, :], past[:, :, :], AX.X, ALU.add))
                    step(dve.tensor_scalar(tile_expert[:, :], texp[:, :], float(EXPERTS - 1), None, ALU.min))

                    def row_of(b, j):
                        dve.tensor_scalar(row[j][:, :], flat(xall[:, ds(b, 1), :]), mv2[:, ds(b, 1), 0], rstd2[:, ds(b, 1)],
                                          ALU.subtract, ALU.mult)
                        dve.tensor_copy(row_slot[j][:, :], slots[:, :, ds(b, 1)].rearrange("p k b -> p (k b)")).then_inc(row_ok, 1)

                    for j in range(BC):
                        row_of(j, j)
                    with dve.Fori(1, BLOCKS // BC) as c:
                        for j in range(BC):
                            dve.wait_ge(sent[j], c * 32)
                            row_of(c * BC + j, j)

        UT = 3
        assert TILES % UT == 0
        work = xall[:, :, :].rearrange("p b d -> p (b d)")
        taken = [0]

        def take(n, count):
            at = [work[:, taken[0] + c * n:taken[0] + (c + 1) * n] for c in range(count)]
            taken[0] += n * count
            return at

        xs, xt, hs, ht, yo = take(DIM, UT), take(KC * P, UT), take(HID, UT), take(HCH * P, UT), take(DIM, UT)
        assert taken[0] <= BLOCKS * DIM
        HCUT = HCH // 2
        with ExitStack() as st:
            w2s = sb(st, "w2s", [P, EXPERTS, HCH * DIM])
            w2s_in = sem("w2s_in")
            ps_h = [ps(st, f"ps_h{n}", [P, 512]) for n in range(4)]
            ps_g = ps(st, "ps_g", [P, 1024])
            ps_t = ps(st, "ps_t3", [P, 512])
            ps_y = ps(st, "ps_y3", [P, 512])
            xs_in = [sem(f"xs_in{v}") for v in range(UT)]
            y_out = [sem(f"y_out{v}") for v in range(UT)]
            xt_ps, xt_sb, h1_ps, h3_ps, silu_ok, h_ok, ht_ps, ht_a, ht_d, y_ps, y_sb = map(sem, (
                "xt3_ps", "xt3_sb", "h1_ps", "h3_ps", "silu_ok", "h_ok", "ht_ps", "ht_a", "ht_d", "y_ps", "y_sb"))

            def after(eng, s, value):
                if not isinstance(value, int) or value > 0:
                    eng.wait_ge(s, value)

            def tiles_in_turn(eng, body):
                last = TILES // UT - 1
                for v in range(UT):
                    body(0, v)
                with eng.Fori(1, last) as i:
                    for v in range(UT):
                        body(i, v)
                for v in range(UT):
                    body(last, v)

            def ht_at(c):
                return c // HCUT * 512 + c % HCUT * P

            with nc.Block() as block:
                @block.sync
                def _(sp):
                    def load(i, v):
                        after(sp, xt_ps, (i - 1) * UT + v + 1)
                        sp.dma_start(xs[v], slots_x[ds((i * UT + v) * P, P), :]).then_inc(xs_in[v], 16)
                    for v in range(UT):
                        load(0, v)
                    for e in range(EXPERTS):
                        sp.dma_start(w2s[:, e, :], w2_t[e].rearrange("p k n -> p (k n)")).then_inc(w2s_in, 16)
                    with sp.Fori(1, TILES // UT) as i:
                        for v in range(UT):
                            wait_apart(sp, xt_ps, (i - 1) * UT + (v + 1), tick)
                            sp.dma_start(xs[v], slots_x[ds((i * UT + v) * P, P), :]).then_inc(xs_in[v], 16)

                @block.gpsimd
                def _(pool):
                    with pool.Fori(0, TILES // UT) as i:
                        for v in range(UT):
                            wait_apart(pool, y_sb, i * UT + (v + 1), tick)
                            pool.dma_start(slots_y[ds((i * UT + v) * P, P), :], yo[v]).then_inc(y_out[v], 16)
                    for v in range(UT):
                        pool.wait_ge(y_out[v], 16 * (TILES // UT))

                @block.scalar
                def _(act):
                    def copy_xt(i, v):
                        act.wait_ge(xt_ps, i * UT + (v + 1))
                        act.copy(xt[v], ps_t[:, 0:KC * P]).then_inc(xt_sb, 1)

                    def finish(i, v):
                        i, v = (i, v - 1) if v else (i - 1, UT - 1)
                        k = i * UT + v
                        act.wait_ge(ht_ps, k + 1)
                        act.copy(ht[v][:, 0:HCUT * P], ps_g[:, 0:HCUT * P]).then_inc(ht_a, 1)
                        return lambda: (act.wait_ge(y_ps, k + 1), after(act, y_out[v], i * 16),
                                        act.copy(yo[v], ps_y[:, 0:DIM]).then_inc(y_sb, 1))

                    def tile(i, v):
                        k = i * UT + v
                        act.wait_ge(h1_ps, k + 1)
                        after(act, ht_ps, k - UT + 1)
                        for n in range(2):
                            last = act.activation(hs[v][:, n * HALF:(n + 1) * HALF], ps_h[n][:, 0:HALF], ACT.Silu)
                        last.then_inc(silu_ok, 1)
                        first_tile = isinstance(i, int) and i == 0 and v == 0
                        last_tile = isinstance(i, int) and k == TILES - 1
                        y_copy = None if first_tile else finish(i, v)
                        if not last_tile:
                            copy_xt(*((i, v + 1) if v + 1 < UT else (i + 1, 0)))
                        if y_copy:
                            y_copy()

                    copy_xt(0, 0)
                    tiles_in_turn(act, tile)
                    finish(TILES // UT, 0)()

                @block.vector
                def _(dve):
                    def finish(i, v):
                        i, v = (i, v - 1) if v else (i - 1, UT - 1)
                        dve.wait_ge(ht_ps, i * UT + (v + 1))
                        n = HCH - 1 - HCUT
                        dve.tensor_copy(ht[v][:, HCUT * P:(HCH - 1) * P], ps_g[:, 512:512 + n * P])
                        dve.tensor_copy(ht[v][0:HLAST, (HCH - 1) * P:HCH * P],
                                        ps_g[0:HLAST, 512 + n * P:512 + (n + 1) * P]).then_inc(ht_d, 1)

                    def tile(i, v):
                        k = i * UT + v
                        if not (isinstance(i, int) and k == 0):
                            finish(i, v)
                        dve.wait_ge(silu_ok, k + 1)
                        dve.wait_ge(h3_ps, k + 1)
                        for n in range(2):
                            cols = hs[v][:, n * HALF:(n + 1) * HALF]
                            last = dve.tensor_tensor(cols, cols, ps_h[2 + n][:, 0:HALF], ALU.mult)
                        last.then_inc(h_ok, 1)

                    tiles_in_turn(dve, tile)
                    finish(TILES // UT, 0)

                @block.tensor
                def _(pe):
                    def turn(i, v):
                        pe.wait_ge(xs_in[v], i * 16 + 16)
                        for k in range(KC):
                            last = pe.transpose(ps_t[:, k * P:(k + 1) * P], xs[v][:, k * P:(k + 1) * P], ident[:, :])
                        last.then_inc(xt_ps, 1)

                    def up(e, v, m, done):
                        for half in range(2):
                            for k in range(KC):
                                at = k * W13 + m * HID + half * HALF
                                last = pe.matmul(ps_h[2 * m + half][:, 0:HALF], xt[v][:, k * P:(k + 1) * P],
                                                 flat(w13[:, ds(e, 1), at:at + HALF]), start=(k == 0), stop=(k == KC - 1))
                        last.then_inc(done, 1)

                    def turn_h(v):
                        for c in range(HCH):
                            w = min(P, HID - c * P)
                            last = pe.transpose(ps_g[0:w, ht_at(c):ht_at(c) + P], hs[v][:, c * P:c * P + w], ident[:, :])
                        last.then_inc(ht_ps, 1)

                    def down(e, v):
                        for c in range(HCH):
                            w = min(P, HID - c * P)
                            last = pe.matmul(ps_y[:, 0:DIM], ht[v][0:w, c * P:(c + 1) * P],
                                             flat(w2s[0:w, ds(e, 1), c * DIM:(c + 1) * DIM]), start=(c == 0), stop=(c == HCH - 1))
                        last.then_inc(y_ps, 1)

                    def expert(k):
                        return pe.value_load(tile_expert[0:1, ds(k, 1)], min_val=0, max_val=EXPERTS - 1)

                    def tile(i, v):
                        k = i * UT + v
                        first_tile = isinstance(i, int) and k == 0
                        last_tile = isinstance(i, int) and k == TILES - 1
                        e = expert(k)
                        pe.wait_ge(xt_sb, k + 1)
                        after(pe, silu_ok, k)
                        up(e, v, 0, h1_ps)
                        u = (v - 1) % UT
                        if not first_tile:
                            pe.wait_ge(h_ok, k)
                            after(pe, ht_a, k - 1)
                            after(pe, ht_d, k - 1)
                            turn_h(u)
                        if not last_tile:
                            turn(*((i, v + 1) if v + 1 < UT else (i + 1, 0)))
                        up(e, v, 1, h3_ps)
                        if not first_tile:
                            e_before = expert(k - 1)
                            pe.wait_ge(ht_a, k)
                            pe.wait_ge(ht_d, k)
                            after(pe, y_sb, k - 1)
                            down(e_before, u)

                    turn(0, 0)
                    pe.wait_ge(w2s_in, 16 * EXPERTS)
                    tiles_in_turn(pe, tile)
                    k = TILES
                    pe.wait_ge(h_ok, k)
                    pe.wait_ge(ht_a, k - 1)
                    pe.wait_ge(ht_d, k - 1)
                    turn_h((k - 1) % UT)
                    e_last = expert(k - 1)
                    pe.wait_ge(ht_a, k)
                    pe.wait_ge(ht_d, k)
                    pe.wait_ge(y_sb, k - 1)
                    down(e_last, (k - 1) % UT)

        UB = 6
        FULL = BLOCKS - 1
        assert FULL % UB == 0
        taken[0] = 0
        ya, yb, xo = take(DIM, UB), take(DIM, UB), take(DIM, UB)
        with ExitStack() as st:
            pair = [sb(st, f"pair{v}", [P, 2], I32) for v in range(UB)]
            y_in, x_in3, o_out = ([sem(f"{n}{v}") for v in range(UB)] for n in ("y_in", "x_in3_", "o_out"))
            pair_ok, mix1, mix2 = sem("pair_ok"), sem("mix1"), sem("mix2")

            def in_turn(eng, body):
                for v in range(UB):
                    body(0, v, v)
                with eng.Fori(1, FULL // UB) as i:
                    for v in range(UB):
                        body(i, v, i * UB + v)
                body(FULL // UB, 0, FULL)

            with nc.Block() as block:
                @block.gpsimd
                def _(pool):
                    def fetch(i, v, b):
                        after(pool, mix2, b - UB + 1)
                        pool.tensor_copy(pair[v][:, :], slots[:, :, ds(b, 1)].rearrange("p k b -> p (k b)")).then_inc(pair_ok, 1)
                        wait_apart(pool, pair_ok, b + 1, tick)
                        for n, y in enumerate((ya, yb)):
                            pool.indirect_dma_start(y[v], None, slots_y,
                                                    bass.IndirectOffsetOnAxis(ap=pair[v][:, n:n + 1], axis=0)).then_inc(y_in[v], 16)
                    in_turn(pool, fetch)

                @block.sync
                def _(sp):
                    def load(i, v, b):
                        if not (isinstance(i, int) and i == 0):
                            wait_apart(sp, o_out[v], i * 16, tick)
                        sp.dma_start(xo[v], x2_dram[ds(b * P, P), :]).then_inc(x_in3[v], 16)
                    in_turn(sp, load)

                @block.vector
                def _(dve):
                    def mix(i, v, b):
                        dve.wait_ge(y_in[v], i * 32 + 32)
                        dve.wait_ge(x_in3[v], i * 16 + 16)
                        dve.scalar_tensor_tensor(xo[v], ya[v], flat(gates[:, 0:1, ds(b, 1)]), xo[v], ALU.mult, ALU.add).then_inc(mix1, 1)
                        dve.wait_ge(mix1, b + 1)
                        dve.scalar_tensor_tensor(xo[v], yb[v], flat(gates[:, 1:2, ds(b, 1)]), xo[v], ALU.mult, ALU.add).then_inc(mix2, 1)
                    in_turn(dve, mix)

                @block.scalar
                def _(act):
                    def store(i, v, b):
                        if isinstance(b, int) and b == FULL:
                            act.wait_ge(mix2, b + 1)
                            act.dma_start(out[FULL * P:NODES, :], xo[v][0:LAST, :]).then_inc(o_out[v], 16)
                        else:
                            wait_apart(act, mix2, b + 1, tick)
                            act.dma_start(out[ds(b * P, P), :], xo[v]).then_inc(o_out[v], 16)
                    in_turn(act, store)
                    for v in range(UB):
                        act.wait_ge(o_out[v], 16 * (FULL // UB + (v == 0)))


_INS = ['x', 'src', 'dst', 'edge_attr_16', 'edge_attr_4', 'L0_gnn_W_n', 'L0_gnn_attn_l', 'L0_gnn_attn_r', 'L0_gnn_attn_m',
        'L0_ffn_router_w', 'L0_ffn_w1', 'L0_ffn_w2', 'L0_ffn_w3']


def kernel(**inputs):
    import numpy as _np
    import concourse.bacc as _bacc
    from concourse import mybir as _mybir
    from concourse.bass_utils import run_bass_kernel_spmd as _run

    nc = _bacc.Bacc("TRN2", target_bir_lowering=False, num_devices=1)
    arrays, args = {}, []
    for name in _INS:
        a = _np.ascontiguousarray(inputs[name])
        arrays[f"in_{name}_dram"] = a
        args.append(nc.dram_tensor(f"in_{name}_dram", a.shape, _mybir.dt.from_np(a.dtype), kind="ExternalInput").ap())
    args.append(nc.dram_tensor("out_0_dram", (NODES, DIM), F32, kind="ExternalOutput").ap())
    gnn_moe_kernel(nc, *args)
    r = _run(nc, [arrays], core_ids=[0])
    return r.results[0]["out_0_dram"]
```

```python
import concourse.bass as bass
from concourse import mybir
from contextlib import ExitStack


F32 = mybir.dt.float32
I32 = mybir.dt.int32
ALU = mybir.AluOpType
ACT = mybir.ActivationFunctionType
AX = mybir.AxisListType
ds = bass.ds

P = 128
NODES, DIM = 6250, 256
EDGES = 200000
HEADS, HDIM, T, F = 8, 32, 4, 16
HT = HEADS * T
EXPERTS, HID = 8, 682
SLOPE, LN_EPS = 0.2, 1e-5

BLOCKS = -(-NODES // P)
LAST = NODES - (BLOCKS - 1) * P
ROWS = BLOCKS * P
COLS = 1568
EROWS = P * COLS
IC = 6
ITEM = IC * P
ITEMS = (EDGES + BLOCKS * (ITEM - 1)) // ITEM + 1
PADDED = EROWS + ITEM
NO_NODE = 8192
BIG = 2.0 ** 100
PW = HEADS * (HDIM + 1)
FD = PW + HT
SUMW = PW + HEADS + 1

KC = DIM // P
HCH = -(-HID // P)
HLAST = HID - (HCH - 1) * P
HALF = HID // 2
W13 = 2 * HID
TILES = (2 * NODES + EXPERTS * (P - 1)) // P
SLOT_TILES = TILES + 2

IV = 5
SLOTS = 2 * IV
ROUNDS = ITEMS // SLOTS
PER_ROUND = 2 * (IV * 3 + 4)
LAG = IV + 2
FILL = -(-SLOT_TILES // (ROUNDS - 2))
assert ROUNDS * SLOTS == ITEMS and EROWS >= EDGES
BC = 7
EARLY = 5
PIECES = 50
PIECE = EDGES // PIECES
assert BLOCKS % BC == 0 and TILES % BC == 0


class Steps:

    def __init__(self, eng, sem):
        self.eng, self.sem, self.base, self.n = eng, sem, 0, 0

    def loop(self, i, per, first=0):
        assert self.per is None
        self.start, self.first, self.i, self.per, self.n = self.base, first, i, per, 0

    def end(self, rounds):
        assert self.n == self.per, (self.n, self.per)
        self.base, self.n, self.per = self.start + rounds * self.per, 0, None

    per = None

    def __call__(self, ins):
        ins.then_inc(self.sem, 1)
        self.n += 1
        if self.per is None:
            self.base += 1
            self.n = 0
            self.eng.wait_ge(self.sem, self.base)
        else:
            self.eng.wait_ge(self.sem, self.i * self.per + (self.start - self.first * self.per + self.n))


def wait_apart(eng, sem, value, tick):
    eng.wait_ge(sem, value)
    eng.sem_inc(tick, 1)


def flat(ap):
    return ap.rearrange("p a n -> p (a n)")


def join_stats(dve, step, stats, mv, tmp, var_ok):
    mean = [stats[:, :, 1], stats[:, :, 4]]
    dve.tensor_tensor(tmp[:, :, 0], mean[0], mean[1], ALU.subtract)
    dve.tensor_tensor(tmp[:, :, 1], stats[:, :, 2], stats[:, :, 5], ALU.add)
    step(dve.tensor_tensor(mv[:, :, 0], mean[0], mean[1], ALU.add))
    dve.tensor_scalar(mv[:, :, 0], mv[:, :, 0], 0.5, None, ALU.mult)
    step(dve.scalar_tensor_tensor(tmp[:, :, 0], tmp[:, :, 0], 0.25, tmp[:, :, 0], ALU.mult, ALU.mult))
    dve.scalar_tensor_tensor(mv[:, :, 1], tmp[:, :, 1], 1.0 / DIM, tmp[:, :, 0], ALU.mult, ALU.add).then_inc(var_ok, 1)
    dve.wait_ge(var_ok, 1)


def node_view(dram):
    return dram.rearrange("(b p) d -> p b d", p=P)


def gnn_moe_kernel(nc, x, src, dst, edge16, edge4, w_n, attn_l, attn_r, attn_m, router_w, w1, w2, w3, out):
    def dram(name, shape, dt=F32):
        return nc.dram_tensor(name, shape, dt, kind="Internal").ap()

    table = dram("table", (ROWS, FD))
    dst_pad = dram("dst_pad", (PADDED,), I32)
    src_pad = dram("src_pad", (PADDED,), I32)
    e16_pad = dram("e16_pad", (PADDED, F))
    e4_pad = dram("e4_pad", (PADDED, T))
    pen_pad = dram("pen_pad", (PADDED,))
    w13_t = dram("w13_t", (EXPERTS, P, KC, W13))
    w2_t = dram("w2_t", (EXPERTS, P, HCH, DIM))
    x2_dram = dram("x2_dram", (ROWS, DIM))
    slots_x = dram("slots_x", (FILL * (ROUNDS - 2) * P, DIM))
    slots_y = dram("slots_y", (SLOT_TILES * P, DIM))

    with ExitStack() as ctx:
        in_steps = []

        def sem(name, lasting=False):
            handle = nc.alloc_semaphore(name=name)
            if not lasting:
                in_steps.append(handle)
            return handle

        def clear_sems():
            nc.clear_and_free_semaphores(in_steps)
            in_steps.clear()
            nc.all_engine_barrier()

        def sb(stack, name, shape, dt=F32):
            return stack.enter_context(nc.sbuf_tensor(name, shape, dt))

        def ps(stack, name, shape):
            return stack.enter_context(nc.psum_tensor(name, shape, F32))

        dve_step, pool_step = (sem(n, lasting=True) for n in ("dve_step", "pool_step"))
        dve_steps = Steps(nc.vector, dve_step)
        tick = sem("tick", lasting=True)

        ident = sb(ctx, "ident", [P, P])
        ones = sb(ctx, "ones", [P, P])
        iota_row = sb(ctx, "iota_row", [P, P])
        part = sb(ctx, "part", [P, 1])
        blk_i = sb(ctx, "blk_i", [1, ITEMS], I32)
        start_i = sb(ctx, "start_i", [1, ITEMS], I32)
        blk128 = sb(ctx, "blk128", [P, ITEMS])
        rt = sb(ctx, "rt", [P, KC, EXPERTS])
        lg = sb(ctx, "lg", [P, BLOCKS, EXPERTS])
        mv2 = sb(ctx, "mv2", [P, BLOCKS, 2])
        rstd2 = sb(ctx, "rstd2", [P, BLOCKS])
        zero_row = sb(ctx, "zero_row", [P, DIM])

        acc = sb(ctx, "acc", [P, BLOCKS + 1, HEADS, HDIM + 1])
        work = acc[:, :, :, :].rearrange("p b h d -> p (b h d)")
        taken = [0]

        def take(n, count):
            at = [work[:, taken[0] + c * n:taken[0] + (c + 1) * n] for c in range(count)]
            taken[0] += n * count
            assert taken[0] <= (BLOCKS + 1) * PW
            return at

        edges_ctx = ctx.enter_context(ExitStack())
        er = sb(edges_ctx, "er", [P, BLOCKS + 1, HT])
        bm = sb(edges_ctx, "bm", [P, 8, HT])
        node_id = sb(edges_ctx, "node_id", [P, ITEMS])

        start_ctx = ctx.enter_context(ExitStack())
        dst_sb = sb(start_ctx, "dst_sb", [P, COLS + 1], I32)
        pen = sb(start_ctx, "pen", [P, COLS])
        junk = sb(start_ctx, "junk", [P, COLS])
        thr = sb(start_ctx, "thr", [P, BLOCKS])
        cnt = sb(start_ctx, "cnt", [P, BLOCKS + 1])
        cnt_ok, copied, pen_out = sem("cnt_ok"), sem("copied"), sem("pen_out")

        with ExitStack() as st:
            xall = sb(st, "xall", [P, BLOCKS, DIM])
            wall = sb(st, "wall", [P, KC, DIM + 2 * HT])
            wn_t = sb(st, "wn_t", [P, KC, DIM])
            bd = sb(st, "bd", [P, KC, 2, HT])
            zeros = sb(st, "zeros", [P, 2048])
            pad_i = sb(st, "pad_i", [64, 64], I32)
            rt_rows = sb(st, "rt_rows", [EXPERTS, DIM])
            stats = sb(st, "stats", [P, BLOCKS, 6])
            mv = sb(st, "mv", [P, BLOCKS, 2])
            tmp = sb(st, "tmp", [P, BLOCKS, 2])
            rstd = sb(st, "rstd", [P, BLOCKS])
            eps = sb(st, "eps", [P, 1])
            xt = sb(st, "xt", [P, 2, KC, P])
            xn = sb(st, "xn", [P, 2, DIM])
            fo = sb(st, "fo", [P, 2, FD])
            ps_w = ps(st, "ps_w", [P, 512])
            ps_t = [ps(st, f"ps_t{i}", [P, 512]) for i in range(2)]
            ps_f = [ps(st, f"ps_f{i}", [P, 512]) for i in range(2)]

            ident_zero, consts, zeroed, x_in, w_in, dst_in, dst_none, pen_ok = map(
                sem, ("ident_zero", "consts", "zeroed", "x_in", "w_in", "dst_in", "dst_none", "pen_ok"))
            fills, pads, wt_ps, wt_sb, wlr_ps, wall_ok = map(sem, ("fills", "pads", "wt_ps", "wt_sb", "wlr_ps", "wall_ok"))
            stats_ok, var_ok, std_ok, xn_ok, xt_ps, xt_sb = map(sem, ("stats_ok", "var_ok", "std_ok", "xn_ok", "xt_ps", "xt_sb"))
            f_ps, f_sb = sem("f_ps"), sem("f_sb")
            f_out = [sem("f_out0"), sem("f_out1")]

            with nc.Block() as block:
                @block.gpsimd
                def _(pool):
                    pool.memset(dst_sb[:, :], NO_NODE).then_inc(dst_none, 1)
                    pool.iota(thr[:, :], pattern=[[P, BLOCKS]], base=P, channel_multiplier=0,
                              allow_small_or_imprecise_dtypes=True).then_inc(dst_none, 1)
                    pool.memset(cnt[:, 0:1], 0.0).then_inc(dst_none, 1)
                    pool.memset(ident[:, :], 0.0).then_inc(ident_zero, 1)
                    pool.memset(ones[:, :], 1.0).then_inc(consts, 1)
                    pool.iota(iota_row[:, :], pattern=[[1, P]], base=0, channel_multiplier=0,
                              allow_small_or_imprecise_dtypes=True).then_inc(consts, 1)
                    pool.iota(part[:, :], pattern=[[0, 1]], base=0, channel_multiplier=1,
                              allow_small_or_imprecise_dtypes=True).then_inc(consts, 1)
                    pool.wait_ge(ident_zero, 1)
                    pool.affine_select(out=ident[:, :], in_=ident[:, :], compare_op=ALU.not_equal, fill=1.0,
                                       base=0, pattern=[[-1, P]], channel_multiplier=1).then_inc(consts, 1)
                    pool.memset(zero_row[:, :], 0.0).then_inc(consts, 1)
                    pool.memset(zeros[:, :], 0.0).then_inc(zeroed, 1)
                    pool.memset(pad_i[:, 0:32], 0).then_inc(zeroed, 1)
                    pool.memset(pad_i[:, 32:64], NO_NODE).then_inc(zeroed, 1)

                @block.sync
                def _(sp):
                    sp.wait_ge(dst_none, 3)
                    sp.dma_start(dst_sb[0:1, 1:COLS + 1], dst[0:COLS].unsqueeze(0)).then_inc(dst_in, 16)
                    full = EDGES // COLS
                    sp.dma_start(dst_sb[1:full, :], bass.AP(dst.tensor, COLS - 1, [(COLS, full - 1), (1, COLS + 1)])).then_inc(dst_in, 16)
                    sp.dma_start(dst_sb[full:P, 0:EDGES - full * COLS + 1], dst[full * COLS - 1:EDGES].unsqueeze(0)).then_inc(dst_in, 16)
                    xv = x[0:(BLOCKS - 1) * P, :].rearrange("(b p) d -> p b d", p=P)
                    sp.dma_start(xall[:, 0:BLOCKS - 1, :], xv).then_inc(x_in, 16)
                    sp.dma_start(wall[:, :, 0:DIM], w_n.rearrange("(k p) d -> p k d", p=P)).then_inc(w_in, 16)
                    sp.dma_start(rt_rows[:, :], router_w).then_inc(w_in, 16)
                    sp.wait_ge(dve_step, 4)
                    sp.dma_start(xall[0:LAST, BLOCKS - 1, :], x[(BLOCKS - 1) * P:NODES, :]).then_inc(x_in, 16)
                    def copy_edges(c):
                        for wide, narrow in ((e16_pad, edge16), (e4_pad, edge4)):
                            sp.dma_start(wide[ds(c * PIECE, PIECE), :].rearrange("(a n) f -> a (n f)", a=16),
                                         narrow[ds(c * PIECE, PIECE), :].rearrange("(a n) f -> a (n f)", a=16)).then_inc(copied, 16)

                    with sp.Fori(0, BLOCKS - 1, 2) as b:
                        for u in range(2):
                            sp.wait_ge(f_sb, b + (u + 1))
                            sp.dma_start(table[ds((b + u) * P, P), :], fo[:, u, :]).then_inc(f_out[u], 16)
                            copy_edges(b + u)
                    sp.wait_ge(f_sb, BLOCKS)
                    sp.dma_start(table[(BLOCKS - 1) * P:ROWS, :], fo[:, 0, :]).then_inc(f_out[0], 16)
                    for c in range(BLOCKS - 1, PIECES):
                        copy_edges(c)
                    sp.wait_ge(f_out[0], 16 * (BLOCKS // 2 + 1))
                    sp.wait_ge(f_out[1], 16 * (BLOCKS // 2))
                    sp.wait_ge(pads, 64)
                    sp.wait_ge(fills, 16 * 3)

                @block.scalar
                def _(act):
                    act.wait_ge(dve_step, 2)
                    for h in range(HEADS):
                        k, r = (h * HDIM) // P, (h * HDIM) % P
                        for s, a in enumerate((attn_l, attn_r)):
                            act.dma_start(bd[r:r + HDIM, k, s, h * T:(h + 1) * T], a[h]).then_inc(w_in, 16)
                    for j in range(8):
                        act.dma_start(bm[j * F:(j + 1) * F, j, :].rearrange("f (h t) -> f h t", h=HEADS),
                                     attn_m.rearrange("h f t -> f h t")).then_inc(w_in, 16)
                    act.dma_start(dst_pad[0:EDGES].rearrange("(a n) -> a n", a=16),
                                  dst.rearrange("(a n) -> a n", a=16)).then_inc(pads, 16)
                    act.dma_start(src_pad[0:EDGES].rearrange("(a n) -> a n", a=16),
                                  src.rearrange("(a n) -> a n", a=16)).then_inc(pads, 16)
                    act.wait_ge(zeroed, 3)
                    n = (PADDED - EDGES) // 64
                    act.dma_start(dst_pad[EDGES:PADDED].rearrange("(a n) -> a n", n=n),
                                  pad_i[:, 32:32 + n]).then_inc(pads, 16)
                    act.dma_start(src_pad[EDGES:PADDED].rearrange("(a n) -> a n", n=n),
                                  pad_i[:, 0:n]).then_inc(pads, 16)
                    act.dma_start(e16_pad[EDGES:PADDED, :].rearrange("(a n) f -> a (n f)", n=n),
                                  zeros[0:64, 0:n * F]).then_inc(fills, 16)
                    act.dma_start(e4_pad[EDGES:PADDED, :].rearrange("(a n) f -> a (n f)", n=n),
                                  zeros[0:64, 0:n * T]).then_inc(fills, 16)
                    act.dma_start(pen_pad[EROWS:PADDED].rearrange("(a n) -> a n", a=P), zeros[:, 0:IC]).then_inc(fills, 16)
                    act.wait_ge(pen_ok, 1)
                    act.dma_start(pen_pad[0:EROWS].rearrange("(p t) -> p t", p=P), pen[:, :]).then_inc(pen_out, 16)
                    act.wait_ge(wt_ps, 1)
                    act.copy(wn_t[:, 0, :], ps_w[:, 0:DIM])
                    act.copy(wn_t[:, 1, :], ps_w[:, DIM:2 * DIM]).then_inc(wt_sb, 1)
                    act.wait_ge(wlr_ps, 1)
                    for k in range(KC):
                        act.copy(wall[:, k, DIM:DIM + 2 * HT], ps_t[k][:, 0:2 * HT])
                    act.copy(rt[:, :, :], ps_f[0][:, 0:KC * EXPERTS].rearrange("p (k e) -> p k e", k=KC)).then_inc(wall_ok, 1)
                    act.wait_ge(var_ok, 1)
                    act.activation(rstd[:, :], mv[:, :, 1], ACT.Sqrt, bias=eps[:, 0:1]).then_inc(std_ok, 1)

                    def copy_xt(b, u):
                        act.wait_ge(xt_ps, b + 1)
                        act.copy(xt[:, u, :, :], ps_t[u][:, 0:KC * P].rearrange("p (k n) -> p k n", k=KC)).then_inc(xt_sb, 1)

                    copy_xt(0, 0)
                    copy_xt(1, 1)
                    with act.Fori(2, BLOCKS - 1, 2) as b:
                        for u in range(2):
                            act.wait_ge(f_ps, b + (u - 1))
                            copy_xt(b + u, u)
                    act.wait_ge(f_ps, BLOCKS - 2)
                    copy_xt(BLOCKS - 1, 0)

                @block.vector
                def _(dve):
                    dve_steps(dve.memset(bd[:, :, :, :], 0.0))
                    dve_steps(dve.memset(bm[:, :, :], 0.0))
                    dve_steps(dve.memset(er[:, BLOCKS, :], 0.0))
                    dve_steps(dve.memset(xall[:, BLOCKS - 1, :], 0.0))
                    dve_steps(dve.memset(eps[:, :], LN_EPS))
                    dve_steps(dve.memset(fo[:, :, :], 0.0))
                    dve.wait_ge(dst_in, 48)
                    dve_steps(dve.memset(dst_sb[0:1, 0:1], -1))
                    dve_steps(dve.tensor_tensor(pen[:, :], dst_sb[:, 1:COLS + 1], dst_sb[:, 0:COLS], ALU.is_equal))
                    dve.tensor_scalar(pen[:, :], pen[:, :], BIG, -BIG, ALU.mult, ALU.add).then_inc(pen_ok, 1)

                    def count(b):
                        dve.tensor_scalar(junk[:, :], dst_sb[:, 1:COLS + 1], thr[:, ds(b, 1)], 0.0, ALU.is_lt, ALU.add,
                                          accum_out=cnt[:, ds(b + 1, 1)]).then_inc(cnt_ok, 1)
                    for b in range(EARLY):
                        count(BLOCKS - EARLY + b)
                        dve.wait_ge(cnt_ok, b + 1)
                    dve.wait_ge(x_in, 32)
                    with dve.Fori(0, BLOCKS // BC) as c:
                        for j in range(BC):
                            dve.bn_stats(flat(stats[:, ds(c * BC + j, 1), :]), flat(xall[:, ds(c * BC + j, 1), :])).then_inc(stats_ok, 1)
                    dve.wait_ge(stats_ok, BLOCKS)
                    join_stats(dve, dve_steps, stats, mv, tmp, var_ok)
                    dve.wait_ge(std_ok, 1)
                    dve_steps(dve.reciprocal(rstd[:, :], rstd[:, :]))

                    def norm(b, u):
                        dve.tensor_scalar(xn[:, u, :], flat(xall[:, ds(b, 1), :]), mv[:, ds(b, 1), 0],
                                          rstd[:, ds(b, 1)], ALU.subtract, ALU.mult).then_inc(xn_ok, 1)

                    def rows_out(b, u):
                        dve.wait_ge(f_ps, b + 1)
                        dve.tensor_copy(fo[:, u, 0:PW].rearrange("p (h d) -> p h d", h=HEADS)[:, :, 0:HDIM],
                                        ps_f[u][:, 0:DIM].rearrange("p (h d) -> p h d", h=HEADS))
                        dve.tensor_copy(fo[:, u, PW:FD], ps_f[u][:, DIM:DIM + HT])
                        dve.tensor_copy(er[:, ds(b, 1), :], ps_f[u][:, DIM + HT:DIM + 2 * HT].unsqueeze(1)).then_inc(f_sb, 1)

                    norm(0, 0)
                    norm(1, 1)
                    for u in range(2):
                        dve.wait_ge(xt_ps, u + 1)
                        norm(2 + u, u)
                        rows_out(u, u)
                    with dve.Fori(2, BLOCKS - 3, 2) as b:
                        for u in range(2):
                            dve.wait_ge(xt_ps, b + (u + 1))
                            norm(b + (2 + u), u)
                            dve.wait_ge(cnt_ok, b + (u + EARLY - 2))
                            count(b + (u - 2))
                            dve.wait_ge(f_out[u], b * 8)
                            rows_out(b + u, u)
                    for b in range(BLOCKS - 3, BLOCKS):
                        if b + 2 < BLOCKS:
                            dve.wait_ge(xt_ps, b + 1)
                            norm(b + 2, b % 2)
                        dve.wait_ge(f_out[b % 2], (b - b % 2) * 8)
                        rows_out(b, b % 2)

                @block.tensor
                def _(pe):
                    pe.wait_ge(consts, 5)
                    pe.wait_ge(w_in, 16 * 26)
                    for k in range(KC):
                        for m in range(KC):
                            last = pe.transpose(ps_w[:, k * DIM + m * P:k * DIM + (m + 1) * P],
                                                wall[:, m, k * P:(k + 1) * P], ident[:, :])
                    last.then_inc(wt_ps, 1)
                    for k in range(KC):
                        pe.transpose(ps_f[0][:, k * EXPERTS:(k + 1) * EXPERTS], rt_rows[:, k * P:(k + 1) * P],
                                     ident[0:EXPERTS, 0:EXPERTS])
                    pe.wait_ge(wt_sb, 1)
                    for m in range(KC):
                        for k in range(KC):
                            last = pe.matmul(ps_t[m][:, 0:2 * HT], wn_t[:, k, m * P:(m + 1) * P],
                                             bd[:, k, :, :].rearrange("p s h -> p (s h)"), start=(k == 0), stop=(k == KC - 1))
                    last.then_inc(wlr_ps, 1)
                    pe.wait_ge(wall_ok, 1)

                    def turn(b, u):
                        pe.wait_ge(xn_ok, b + 1)
                        for k in range(KC):
                            last = pe.transpose(ps_t[u][:, k * P:(k + 1) * P],
                                                xn[:, u, k * P:(k + 1) * P], ident[:, :])
                        last.then_inc(xt_ps, 1)

                    def project(u):
                        for k in range(KC):
                            last = pe.matmul(ps_f[u][:, 0:DIM + 2 * HT], xt[:, u, k, :], wall[:, k, :],
                                             start=(k == 0), stop=(k == KC - 1))
                        last.then_inc(f_ps, 1)

                    turn(0, 0)
                    turn(1, 1)
                    for u in range(2):
                        pe.wait_ge(xt_sb, u + 1)
                        turn(2 + u, u)
                        project(u)
                    with pe.Fori(2, BLOCKS - 3, 2) as b:
                        for u in range(2):
                            pe.wait_ge(xt_sb, b + (u + 1))
                            turn(b + (2 + u), u)
                            pe.wait_ge(f_sb, b + (u - 1))
                            project(u)
                    for b in range(BLOCKS - 3, BLOCKS):
                        pe.wait_ge(xt_sb, b + 1)
                        if b + 2 < BLOCKS:
                            turn(b + 2, b % 2)
                        pe.wait_ge(f_sb, b - 1)
                        project(b % 2)

        with ExitStack() as st:
            steps_k = sb(st, "steps_k", [P, ITEMS])
            tri = sb(st, "tri", [P, BLOCKS])
            w_iota = sb(st, "w_iota", [P, ITEMS])
            se = sb(st, "se", [BLOCKS, 2])
            nblk = sb(st, "nblk", [BLOCKS, 1])
            nit = sb(st, "nit", [BLOCKS, 1])
            cend = sb(st, "cend", [BLOCKS, 1])
            dq = sb(st, "dq", [BLOCKS, 1])
            passed = sb(st, "passed", [BLOCKS, ITEMS])
            start_f = sb(st, "start_f", [1, ITEMS])
            wrow = [[sb(st, f"wrow{m}{i}", [P, HCH, DIM]) for i in range(2)] for m in range(2)]
            w2row = [sb(st, f"w2row{i}", [P, KC, HID]) for i in range(2)]
            w13o = [sb(st, f"w13o{i}", [P, KC, W13]) for i in range(2)]
            w2o = [sb(st, f"w2o{i}", [P, HCH, DIM]) for i in range(2)]
            ps_c = ps(st, "ps_c", [P, 512])
            ps_b = ps(st, "ps_b", [P, 1024])
            ps_wt = [ps(st, f"ps_wt{i}", [P, 1024]) for i in range(2)]

            b_const, se_ps, nit_ok, cend_ps, passed_ok, list_ps = map(
                sem, ("b_const", "se_ps", "nit_ok", "cend_ps", "passed_ok", "list_ps"))
            wrow_in = [sem("wrow_in0"), sem("wrow_in1")]
            w_out = [sem("w_out0"), sem("w_out1")]
            turned, turned_sb, out_free = sem("turned"), sem("turned_sb"), [sem("out_free0"), sem("out_free1")]
            TURNS = 2 * KC + HCH // 2

            def weight_turns(u):
                for m in range(2):
                    for k in range(KC):
                        yield [(c * P, P, wrow[m][u][0:(P if c < HCH - 1 else HLAST), c, k * P:(k + 1) * P]) for c in range(HCH)]
                for c2 in range(HCH // 2):
                    yield [((c % 2) * 512 + k * P, P if c < HCH - 1 else HLAST,
                            w2row[u][:, k, c * P:min((c + 1) * P, HID)]) for c in (2 * c2, 2 * c2 + 1) for k in range(KC)]

            with nc.Block() as block:
                @block.sync
                def _(sp):
                    full = (HCH - 1) * P
                    with sp.Fori(0, EXPERTS // 2) as i:
                        for u in range(2):
                            sp.wait_ge(turned, i * (2 * TURNS) + (u + 1) * TURNS)
                            e = i * 2 + u
                            for m, w in enumerate((w1, w3)):
                                sp.dma_start(wrow[m][u][:, 0:HCH - 1, :],
                                             w[ds(e, 1), 0:full, :].rearrange("a (c p) d -> p (a c) d", p=P)).then_inc(wrow_in[u], 16)
                                sp.dma_start(wrow[m][u][0:HLAST, HCH - 1, :],
                                             w[ds(e, 1), full:HID, :].rearrange("a p d -> (a p) d")).then_inc(wrow_in[u], 16)
                            sp.dma_start(w2row[u][:, :, :],
                                         w2[ds(e, 1), :, :].rearrange("a (k p) h -> p (a k) h", p=P)).then_inc(wrow_in[u], 16)

                @block.gpsimd
                def _(pool):
                    pool.memset(tri[:, :], 1.0).then_inc(pool_step, 1)
                    pool.wait_ge(pool_step, 1)
                    pool.affine_select(out=tri[:, :], in_=tri[:, :], compare_op=ALU.is_ge, fill=0.0, base=0,
                                       pattern=[[1, BLOCKS]], channel_multiplier=-1).then_inc(b_const, 1)
                    pool.iota(w_iota[:, :], pattern=[[1, ITEMS]], base=0, channel_multiplier=0,
                              allow_small_or_imprecise_dtypes=True).then_inc(b_const, 1)
                    for u in range(2):
                        pool.memset(w2o[u][:, HCH - 1, :], 0.0).then_inc(out_free[u], 1)
                    with pool.Fori(0, EXPERTS // 2) as i:
                        for u in range(2):
                            e = i * 2 + u
                            for m in range(2):
                                pool.wait_ge(turned_sb, i * (2 * TURNS) + (u * TURNS + (m + 1) * KC + 2))
                                pool.dma_start(w13_t[ds(e, 1), :, :, m * HID:(m + 1) * HID].rearrange("a p k n -> (a p) k n"),
                                               w13o[u][:, :, m * HID:(m + 1) * HID]).then_inc(w_out[u], 16)
                            pool.wait_ge(turned_sb, i * (2 * TURNS) + ((u + 1) * TURNS + 2))
                            pool.dma_start(w2_t[ds(e, 1), :, :, :].rearrange("a p k n -> (a p) k n"), w2o[u][:, :, :]).then_inc(w_out[u], 16)
                            pool.wait_ge(w_out[u], i * 48 + 48)
                            pool.sem_inc(out_free[u], 1)

                @block.vector
                def _(dve):
                    dve.wait_ge(b_const, 2)
                    dve.wait_ge(se_ps, 1)
                    dve_steps(dve.tensor_copy(se[:, :], ps_c[0:BLOCKS, 0:2]))
                    dve_steps(dve.tensor_tensor(nblk[:, :], se[:, 1:2], se[:, 0:1], ALU.subtract))
                    dve_steps(dve.tensor_scalar(steps_k[:, :], w_iota[:, :], float(ITEM), None, ALU.mult))
                    dve_steps(dve.tensor_scalar(passed[:, :], steps_k[0:BLOCKS, :], nblk[:, :], 0.0, ALU.is_lt, ALU.add,
                                                accum_out=nit[:, :]))
                    dve.scalar_tensor_tensor(dq[:, :], nit[:, :], -float(ITEM), nblk[:, :], ALU.mult, ALU.add).then_inc(nit_ok, 1)
                    dve.wait_ge(cend_ps, 1)
                    dve_steps(dve.tensor_copy(cend[:, :], ps_c[0:BLOCKS, 8:9]))
                    dve.tensor_scalar(passed[:, :], w_iota[0:BLOCKS, :], cend[:, :], None, ALU.is_ge).then_inc(passed_ok, 1)
                    dve.wait_ge(list_ps, 1)
                    dve_steps(dve.tensor_copy(blk_i[:, :], ps_c[0:1, 16:16 + ITEMS]))
                    dve_steps(dve.tensor_scalar(blk128[:, :], ps_b[:, 0:ITEMS], float(P), None, ALU.mult))
                    dve_steps(dve.scalar_tensor_tensor(start_f[:, :], w_iota[0:1, :], float(ITEM), ps_b[0:1, 512:512 + ITEMS],
                                                       ALU.mult, ALU.add))
                    dve_steps(dve.tensor_scalar(start_i[:, :], start_f[:, :], float(EDGES), None, ALU.min))
                    dve_steps(dve.tensor_scalar(node_id[:, :], blk128[:, :], part[:, 0:1], None, ALU.add))

                @block.tensor
                def _(pe):
                    pe.sem_inc(turned, 2 * TURNS)
                    with pe.Fori(0, EXPERTS // 2) as i:
                        for u in range(2):
                            pe.wait_ge(wrow_in[u], i * 80 + 80)
                            for n, outs in enumerate(weight_turns(u)):
                                pe.wait_ge(turned_sb, i * (2 * TURNS) + (u * TURNS + n + 1))
                                tile = ps_wt[(u * TURNS + n) % 2]
                                for o, w, rows in outs:
                                    k = rows.shape[0]
                                    last = pe.transpose(tile[0:w, o:o + k], rows, ident[0:k, 0:k])
                                last.then_inc(turned, 1)
                    pe.wait_ge(cnt_ok, BLOCKS)
                    pe.matmul(ps_c[0:BLOCKS, 0:1], cnt[:, 0:BLOCKS], ones[:, 0:1], start=True, stop=True)
                    pe.matmul(ps_c[0:BLOCKS, 1:2], cnt[:, 1:BLOCKS + 1], ones[:, 0:1], start=True, stop=True).then_inc(se_ps, 1)
                    pe.wait_ge(nit_ok, 1)
                    pe.matmul(ps_c[0:BLOCKS, 8:9], tri[0:BLOCKS, :], nit[:, :], start=True, stop=True).then_inc(cend_ps, 1)
                    pe.wait_ge(passed_ok, 1)
                    pe.matmul(ps_c[0:1, 16:16 + ITEMS], ones[0:BLOCKS, 0:1], passed[:, :], start=True, stop=True)
                    pe.matmul(ps_b[:, 0:ITEMS], ones[0:BLOCKS, :], passed[:, :], start=True, stop=True)
                    pe.matmul(ps_b[0:1, 512:512 + ITEMS], dq[:, :], passed[:, :], start=True, stop=True).then_inc(list_ps, 1)

                @block.scalar
                def _(act):
                    act.sem_inc(turned_sb, 2)
                    with act.Fori(0, EXPERTS // 2) as i:
                        for u in range(2):
                            act.wait_ge(out_free[u], i + 1)
                            for n in range(TURNS):
                                act.wait_ge(turned, i * (2 * TURNS) + (2 * TURNS + u * TURNS + n + 1))
                                tile = ps_wt[(u * TURNS + n) % 2]
                                if n < 2 * KC:
                                    m, k = divmod(n, KC)
                                    last = act.copy(w13o[u][:, k, m * HID:(m + 1) * HID], tile[:, 0:HID])
                                else:
                                    c = 2 * (n - 2 * KC)
                                    if c + 1 < HCH - 1:
                                        last = act.copy(w2o[u][:, c:c + 2, :],
                                                        tile[:, :].rearrange("p (c d) -> p c d", c=2)[:, :, 0:DIM])
                                    else:
                                        act.copy(w2o[u][:, c, :], tile[:, 0:DIM])
                                        last = act.copy(w2o[u][0:HLAST, c + 1, :], tile[0:HLAST, 512:512 + DIM])
                                last.then_inc(turned_sb, 1)
                    act.wait_ge(pen_out, 16)
                    act.wait_ge(copied, 32 * PIECES)

        start_ctx.close()

        with ExitStack() as st:
            top_of = sb(st, "top_of", [P, BLOCKS + 1, HEADS])
            rows = [sb(st, f"rows{w}", [P, IV, IC, FD]) for w in range(2)]
            idx = [sb(st, f"idx{s}", [P, IC], I32) for s in range(SLOTS)]
            dst_e = [sb(st, f"dst_e{w}", [P, IV, IC], I32) for w in range(2)]
            neg_rel = [sb(st, f"neg_rel{w}", [P, IV, IC]) for w in range(2)]
            e16 = [sb(st, f"e16_{s}", [P, IC, F]) for s in range(SLOTS)]
            mask = [sb(st, f"mask{w}", [P, IV, IC, T]) for w in range(2)]
            pen_e = [sb(st, f"pen_e{w}", [P, IV, IC]) for w in range(2)]
            dst_row = [sb(st, f"dst_row{v}", [P, ITEM], I32) for v in range(IV)]
            hot_t = [sb(st, f"hot_t{u}", [P, ITEM]) for u in range(2)]
            hot = [sb(st, f"hot{u}", [P, IC, P]) for u in range(2)]
            e16_t = [sb(st, f"e16_t{u}", [IC * F, P]) for u in range(2)]
            term = sb(st, "term", [P, IV, IC, HT])
            summed = sb(st, "summed", [P, IV, IC, HEADS])
            score = [sb(st, f"score{w}", [P, IC, IV, HEADS]) for w in range(2)]
            weight = [sb(st, f"weight{w}", [P, IV, IC, HEADS]) for w in range(2)]
            pen_t = [sb(st, f"pen_t{w}", [IV * HEADS, ITEM + 1]) for w in range(2)]
            e_t = sb(st, "e_t", [IV * HEADS, ITEM])
            top_t = sb(st, "top_t", [IV * HEADS, ITEM])
            head_mark = sb(st, "head_mark", [P, IV, IC])
            begins = sb(st, "begins", [P, IV, IC])
            seen_b = [sb(st, f"seen_b{u}", [P, 1]) for u in range(2)]
            top_new = [sb(st, f"top_new{u}", [P, HEADS]) for u in range(2)]
            less = [sb(st, f"less{u}", [P, 2, HEADS]) for u in range(2)]
            scale = [sb(st, f"scale{u}", [P, 2, HEADS]) for u in range(2)]
            part_sum = sb(st, "part_sum", [P, HEADS, HDIM + 1])
            ps_e16 = [ps(st, f"ps_e16{u}", [P, 512]) for u in range(2)]
            ps_term = [ps(st, f"ps_term{u}", [P, 512]) for u in range(2)]
            ps_acc = [ps(st, f"ps_acc{u}", [P, 512]) for u in range(2)]
            ps_x = ps(st, "ps_x", [P, 1024])
            QH = IV * HEADS

            def flat_edges(ap):
                return ap.rearrange("p v j n -> p (v j) n")

            (pen_end, item_made, rel_ok, term_ps, term_used, e16_ps, e16_sb, summed_ok, scored, xs_ps, et_ok, less_max, exp_ok,
             back_ps, tops_ok, tops_used, begins_ok, msg_ok, square_ok, hot_ok, acc_done, acc_used, less_ok, scale_ok, scaled, added, slots_zero) = map(sem, (
                 "pen_end", "item_made", "rel_ok", "term_ps", "term_used", "e16_ps", "e16_sb", "summed_ok", "scored", "xs_ps", "et_ok",
                 "less_max", "exp_ok", "back_ps", "tops_ok", "tops_used", "begins_ok", "msg_ok", "square_ok", "hot_ok", "acc_done",
                 "acc_used", "less_ok", "scale_ok", "scaled", "added", "slots_zero"))
            gathered, idx_in, item_in = ([sem(f"{n}{s}") for s in range(SLOTS)] for n in ("gathered", "idx_in", "item_in"))
            dst_row_in = [sem(f"dst_row_in{v}") for v in range(IV)]
            pen_in = [sem(f"pen_in{w}") for w in range(2)]
            ITEM_MADE0, TERM_PS0, TERM_USED0, E16_SB0, TOPS_USED0, BEGINS0 = IV, 2, 2, 2, 1, 2
            HOT0, ACC_DONE0, ACC_USED0, ADDED0 = SLOTS, SLOTS, 2, 1

            def number(i, w, v, off=0):
                return i * SLOTS + (w * IV + v + off)

            def slot_of(i, w, v, off=0):
                at = w * IV + v + off
                return at % SLOTS, i + at // SLOTS

            def is_item(k):
                return not isinstance(k, int) or 0 <= k < ITEMS

            def is_batch(n):
                return not isinstance(n, int) or 0 <= n < 2 * ROUNDS

            def all_batches(body, eng, steps=None, behind=0):
                for w in range(2):
                    body(0, w)
                with eng.Fori(1, ROUNDS - 1) as i:
                    if steps:
                        steps.loop(i, PER_ROUND, 1)
                    for w in range(2):
                        body(i, w)
                if steps:
                    steps.end(ROUNDS - 2)
                for i in range(ROUNDS - 1, ROUNDS + behind):
                    for w in range(2):
                        body(i, w)

            with nc.Block() as block:
                @block.sync
                def _(sp):
                    def batch(i, w):
                        n = i * 2 + w
                        wait_apart(sp, begins_ok, n + 1, tick)
                        starts = []
                        for v in range(IV):
                            s = w * IV + v
                            k0 = sp.value_load(start_i[0:1, ds(number(i, w, v), 1)], min_val=0, max_val=EDGES)
                            starts.append(k0)
                            sp.dma_start(idx[s][:, :], src_pad[ds(k0, ITEM)].rearrange("(p j) -> p j", p=P)).then_inc(idx_in[s], 16)
                        for v, k0 in enumerate(starts):
                            s = w * IV + v
                            sp.dma_start(e16[s][:, :, :], e16_pad[ds(k0, ITEM), :].rearrange("(p j) f -> p j f", p=P)).then_inc(item_in[s], 16)
                            sp.dma_start(dst_e[w][:, v, :], dst_pad[ds(k0, ITEM)].rearrange("(p j) -> p j", p=P)).then_inc(item_in[s], 16)
                            sp.dma_start(mask[w][:, v, :, :], e4_pad[ds(k0, ITEM), :].rearrange("(p j) f -> p j f", p=P)).then_inc(item_in[s], 16)
                            sp.dma_start(pen_e[w][:, v, :], pen_pad[ds(k0, ITEM)].rearrange("(p j) -> p j", p=P)).then_inc(item_in[s], 16)
                            sp.dma_start(pen_t[w][v * HEADS:(v + 1) * HEADS, 0:ITEM],
                                         pen_pad[ds(k0, ITEM)].partition_broadcast(HEADS)).then_inc(pen_in[w], 16)
                            wait_apart(sp, item_made, number(i, w, v, 1), tick)
                            sp.dma_start(dst_row[v][:, :], dst_pad[ds(k0, ITEM)].partition_broadcast(P)).then_inc(dst_row_in[v], 16)
                    all_batches(batch, sp)

                @block.gpsimd
                def _(pool):
                    def batch(i, w):
                        for v in range(IV):
                            s = w * IV + v
                            pool.wait_ge(idx_in[s], i * 16 + 16)
                            wait_apart(pool, acc_done, number(i, w, v, 1), tick)
                            for j in range(IC):
                                pool.indirect_dma_start(rows[w][:, v, j, :], None, table,
                                                        bass.IndirectOffsetOnAxis(ap=idx[s][:, j:j + 1], axis=0)).then_inc(gathered[s], 16)
                    all_batches(batch, pool)

                @block.tensor
                def _(pe):
                    pe.sem_inc(acc_done, ACC_DONE0)
                    pe.sem_inc(term_ps, TERM_PS0)

                    def turn_e16(i, w, v, off):
                        k1, (s, it) = number(i, w, v, off + 1), slot_of(i, w, v, off)
                        pe.wait_ge(item_in[s], it * 64 + 64)
                        pe.wait_ge(e16_sb, k1)
                        pe.transpose(ps_e16[s % 2][0:IC * F, 0:P], e16[s][:, :, :].rearrange("p j f -> p (j f)"), ident[:, :]).then_inc(e16_ps, 1)

                    def terms(i, w, v, off):
                        k1, (s, it) = number(i, w, v, off + 1), slot_of(i, w, v, off)
                        tile = ps_term[s % 2]
                        b = pe.value_load(blk_i[0:1, ds(number(i, w, v, off), 1)], min_val=0, max_val=BLOCKS)
                        pe.wait_ge(e16_sb, k1 + E16_SB0)
                        pe.wait_ge(term_used, k1)
                        pe.matmul(tile[:, 0:IC * HT], e16_t[s % 2][:, :], bm[0:IC * F, 0:IC, :].rearrange("p t d -> p (t d)"),
                                  start=True, stop=False)
                        pe.wait_ge(item_made, k1 + ITEM_MADE0)
                        for j in range(IC):
                            last = pe.matmul(tile[:, j * HT:(j + 1) * HT], hot_t[s % 2][:, j::IC], flat(er[:, ds(b, 1), :]),
                                             start=False, stop=(j == IC - 1))
                        last.then_inc(term_ps, 1)

                    def sums(i, w, v, off):
                        k1, (s, it) = number(i, w, v, off + 1), slot_of(i, w, v, off)
                        pe.wait_ge(msg_ok, k1)
                        pe.wait_ge(hot_ok, k1 + HOT0)
                        pe.wait_ge(acc_used, k1)
                        for j in range(IC):
                            last = pe.matmul(ps_acc[s % 2][:, 0:SUMW], hot[s % 2][:, j, :], rows[s // IV][:, s % IV, j, 0:SUMW],
                                             start=(j == 0), stop=(j == IC - 1))
                        last.then_inc(acc_done, 1)

                    def back(n):
                        wait_apart(pe, tops_ok, n + 1, tick)
                        for j in range(IC):
                            last = pe.transpose(ps_x[:, j * QH:(j + 1) * QH], top_t[:, j::IC], ident[0:QH, 0:QH])
                        last.then_inc(back_ps, 1)

                    def turn_scores(n, w):
                        pe.wait_ge(tops_used, n + 1)
                        wait_apart(pe, scored, n + 1, tick)
                        for j in range(IC):
                            last = pe.transpose(ps_x[0:QH, j * P:(j + 1) * P], score[w][:, j, :, :].rearrange("p v h -> p (v h)"), ident[:, :])
                        last.then_inc(xs_ps, 1)

                    def batch(i, w):
                        before = i * 2 + w - 1
                        for v in range(IV):
                            if v == 1 and is_batch(before):
                                back(before)
                            if is_item(number(i, w, v, 1)):
                                terms(i, w, v, 1)
                            if is_item(number(i, w, v, 2)):
                                turn_e16(i, w, v, 2)
                            if v == 0 and is_batch(before):
                                turn_scores(before, 1 - w)
                            if is_item(number(i, w, v, -LAG)):
                                sums(i, w, v, -LAG)

                    for v in range(2):
                        turn_e16(0, 0, v, 0)
                    terms(0, 0, 0, 0)
                    all_batches(batch, pe, behind=1)

                @block.scalar
                def _(act):
                    act.sem_inc(e16_sb, E16_SB0)
                    act.sem_inc(hot_ok, HOT0)

                    def copy_e16(i, w, v, off):
                        k1, (s, it) = number(i, w, v, off + 1), slot_of(i, w, v, off)
                        act.wait_ge(e16_ps, k1)
                        act.wait_ge(term_ps, k1)
                        act.copy(e16_t[s % 2][:, :], ps_e16[s % 2][0:IC * F, 0:P]).then_inc(e16_sb, 1)

                    def one_hot(i, w, v, off):
                        k1, (s, it) = number(i, w, v, off + 1), slot_of(i, w, v, off)
                        act.wait_ge(rel_ok, it * 2 + (s // IV + 1))
                        act.wait_ge(acc_done, k1 + (ACC_DONE0 - 2))
                        for j in range(IC):
                            last = act.activation(hot[s % 2][:, j, :], iota_row[:, :], ACT.Square, bias=neg_rel[s // IV][:, s % IV, j:j + 1])
                        last.then_inc(square_ok, 1)
                        act.wait_ge(square_ok, k1)
                        act.activation(hot[s % 2][:, :, :], hot[s % 2][:, :, :], ACT.Relu, bias=1.0, scale=-1.0).then_inc(hot_ok, 1)

                    def scales(i, w, v, off):
                        k1, (s, it) = number(i, w, v, off + 1), slot_of(i, w, v, off)
                        act.wait_ge(less_ok, k1)
                        act.activation(scale[s % 2][:, :, :], less[s % 2][:, :, :], ACT.Exp, scale=1.0 / 3.0).then_inc(scale_ok, 1)

                    def scale_sums(i, w, v, off):
                        k1, (s, it) = number(i, w, v, off + 1), slot_of(i, w, v, off)
                        b = act.value_load(blk_i[0:1, ds(number(i, w, v, off), 1)], min_val=0, max_val=BLOCKS)
                        act.wait_ge(scale_ok, k1)
                        act.wait_ge(added, k1)
                        for h in range(HEADS):
                            so_far = flat(acc[:, ds(b, 1), h, :])
                            last = act.activation(so_far, so_far, ACT.Copy, scale=scale[s % 2][:, 0, h:h + 1])
                        last.then_inc(scaled, 1)

                    def exp_batch(n, w):
                        act.wait_ge(less_max, n + 1)
                        p_at = flat_edges(rows[w][:, :, :, 0:PW]).rearrange("p e (h d) -> p e h d", h=HEADS)[:, :, :, HDIM]
                        act.activation(p_at, flat_edges(weight[w][:, :, :, :]), ACT.Exp, scale=1.0 / 3.0).then_inc(exp_ok, 1)

                    def batch(i, w):
                        before = i * 2 + w - 1
                        if w == 0 and not isinstance(i, int):
                            act.dma_start(slots_x[ds((i - 1) * (FILL * P), FILL * P), :].rearrange("(p j) d -> p j d", p=P),
                                          zero_row[:, :].unsqueeze(1).to_broadcast([P, FILL, DIM])).then_inc(slots_zero, 16)
                        for v in range(IV):
                            if v == 0 and is_batch(before):
                                act.wait_ge(summed_ok, before + 1)
                                act.copy(score[1 - w][:, :, :, :], summed[:, :, :, :].rearrange("p v j h -> p j v h")).then_inc(scored, 1)
                            if is_item(number(i, w, v, 2)):
                                copy_e16(i, w, v, 2)
                            if is_item(number(i, w, v, 1 - LAG)):
                                one_hot(i, w, v, 1 - LAG)
                            if v == 0 and is_batch(before):
                                act.wait_ge(xs_ps, before + 1)
                                act.copy(e_t[:, :].rearrange("q (p j) -> q j p", j=IC), ps_x[0:QH, 0:IC * P].rearrange("q (j p) -> q j p", j=IC)).then_inc(et_ok, 1)
                            if is_item(number(i, w, v, -LAG - 1)):
                                scales(i, w, v, -LAG - 1)
                            if v == 1 and is_batch(before):
                                exp_batch(before, 1 - w)
                            if is_item(number(i, w, v, -LAG - 1)):
                                scale_sums(i, w, v, -LAG - 1)

                    act.dma_start(slots_y[TILES * P:SLOT_TILES * P, :].rearrange("(p j) d -> p j d", p=P),
                                  zero_row[:, :].unsqueeze(1).to_broadcast([P, 2, DIM])).then_inc(slots_zero, 16)
                    for v in range(2):
                        copy_e16(0, 0, v, 0)
                    all_batches(batch, act, behind=1)
                    act.wait_ge(slots_zero, 16 * (ROUNDS - 2 + 1))

                @block.vector
                def _(dve):
                    step = dve_steps
                    dve.sem_inc(item_made, ITEM_MADE0)
                    dve.sem_inc(term_used, TERM_USED0)
                    dve.sem_inc(begins_ok, BEGINS0)
                    dve.sem_inc(acc_used, ACC_USED0)
                    dve.sem_inc(tops_used, TOPS_USED0)
                    for w in range(2):
                        dve.memset(pen_t[w][:, ITEM:ITEM + 1], 0.0).then_inc(pen_end, 1)
                    dve.wait_ge(pen_end, 2)
                    step(dve.memset(head_mark[:, :, :], 0.0))
                    step(dve.memset(head_mark[0:1, :, 0:1], 1.0))
                    step(dve.memset(acc[:, :, :, :], 0.0))
                    step(dve.memset(top_of[:, :, :], -BIG))
                    dve.sem_inc(added, ADDED0)

                    def compare(i, w, v, off):
                        k, k1, (s, it) = number(i, w, v, off), number(i, w, v, off + 1), slot_of(i, w, v, off)
                        dve.wait_ge(dst_row_in[s % IV], it * 32 + (s // IV + 1) * 16)
                        dve.wait_ge(term_ps, k1)
                        dve.tensor_scalar(hot_t[s % 2][:, :], dst_row[s % IV][:, :], node_id[:, ds(k, 1)], None,
                                          ALU.is_equal).then_inc(item_made, 1)

                    def relate(i, w):
                        n = i * 2 + w
                        for s in range(w * IV, (w + 1) * IV):
                            dve.wait_ge(item_in[s], i * 64 + 64)
                        dve.wait_ge(hot_ok, n * IV + IV)
                        dve.tensor_tensor(neg_rel[w][:, :, :], blk128[:, ds(n * IV, IV)].unsqueeze(2).to_broadcast([P, IV, IC]),
                                          dst_e[w][:, :, :], ALU.subtract).then_inc(rel_ok, 1)

                    def left_and_right(i, w, v):
                        k1, s = number(i, w, v, 1), w * IV + v
                        dve.wait_ge(term_ps, k1 + TERM_PS0)
                        dve.wait_ge(gathered[s], i * (16 * IC) + 16 * IC)
                        dve.tensor_tensor(term[:, v, :, :], ps_term[s % 2][:, 0:IC * HT].rearrange("p (j d) -> p j d", j=IC),
                                          rows[w][:, v, :, PW:FD], ALU.add).then_inc(term_used, 1)

                    def scores(i, w):
                        n = i * 2 + w
                        dve.wait_ge(term_used, n * IV + (IV + TERM_USED0))
                        masked = flat_edges(term[:, :, :, :]).rearrange("p e (h t) -> p e h t", h=HEADS)
                        step(dve.tensor_tensor(masked, masked, flat_edges(mask[w][:, :, :, :]).unsqueeze(2).to_broadcast([P, IV * IC, HEADS, T]),
                                               ALU.mult))
                        step(dve.tensor_reduce(flat_edges(summed[:, :, :, :]), masked, AX.X, ALU.add))
                        s3 = summed[:, :, :, :].rearrange("p v j h -> p (v j h)")
                        dve.scalar_tensor_tensor(s3, s3, SLOPE, s3, ALU.mult, ALU.max).then_inc(summed_ok, 1)

                    def tops(n, i, w):
                        dve.wait_ge(et_ok, n + 1)
                        dve.wait_ge(pen_in[w], i * (16 * IV) + 16 * IV)
                        step(dve.tensor_tensor_scan(top_t[:, :], pen_t[w][:, 0:ITEM], e_t[:, :], -BIG, ALU.add, ALU.max))
                        dve.tensor_tensor_scan(top_t[:, ::-1], pen_t[w][:, 1:ITEM + 1][:, ::-1], top_t[:, ::-1], -BIG, ALU.add, ALU.max).then_inc(tops_ok, 1)
                        dve.scalar_tensor_tensor(begins[:, :, :], pen_e[w][:, :, :], -1.0 / BIG, head_mark[:, :, :],
                                                 ALU.mult, ALU.max).then_inc(begins_ok, 1)
                        dve.wait_ge(begins_ok, n + 1 + BEGINS0)

                    def below_top(n, w):
                        dve.wait_ge(scored, n + 1)
                        dve.wait_ge(back_ps, n + 1)
                        top = ps_x[:, 0:IC * QH].rearrange("p (j v h) -> p j v h", j=IC, v=IV)
                        dve.tensor_tensor(weight[w][:, :, :, :].rearrange("p v j h -> p j v h"), score[w][:, :, :, :], top,
                                          ALU.subtract).then_inc(less_max, 1)
                        dve.tensor_tensor(rows[w][:, :, :, PW:PW + HEADS], top.rearrange("p j v h -> p v j h"),
                                          begins[:, :, :].unsqueeze(3).to_broadcast([P, IV, IC, HEADS]), ALU.mult).then_inc(tops_used, 1)
                        step(dve.tensor_copy(rows[w][:, :, :, PW + HEADS], begins[:, :, :]))

                    def weigh(i, w, v, off):
                        k1, (s, it) = number(i, w, v, off + 1), slot_of(i, w, v, off)
                        r = rows[s // IV][:, s % IV, :, 0:PW].rearrange("p j (h d) -> p j h d", h=HEADS)[:, :, :, 0:HDIM]
                        p4 = rows[s // IV][:, s % IV, :, 0:PW].rearrange("p j (h d) -> p j h d", h=HEADS)[:, :, :, HDIM:HDIM + 1].to_broadcast([P, IC, HEADS, HDIM])
                        dve.tensor_tensor(r, r, p4, ALU.mult).then_inc(msg_ok, 1)

                    def block_of(i, w, v, off):
                        return dve.value_load(blk_i[0:1, ds(number(i, w, v, off), 1)], min_val=0, max_val=BLOCKS)

                    def meet(i, w, v, off, b):
                        k1, (s, it) = number(i, w, v, off + 1), slot_of(i, w, v, off)
                        u = s % 2
                        here = flat(top_of[:, ds(b, 1), :])
                        item_top = ps_acc[u][:, PW:PW + HEADS]
                        dve.wait_ge(acc_done, k1 + ACC_DONE0)
                        step(dve.tensor_scalar(seen_b[u][:, :], ps_acc[u][:, PW + HEADS:SUMW], BIG, -BIG, ALU.mult, ALU.add))
                        step(dve.scalar_tensor_tensor(top_new[u][:, :], item_top, seen_b[u][:, :], here, ALU.add, ALU.max))
                        dve.scalar_tensor_tensor(less[u][:, 1, :], item_top, seen_b[u][:, :], top_new[u][:, :], ALU.add, ALU.subtract)
                        dve.tensor_tensor(less[u][:, 0, :], here, top_new[u][:, :], ALU.subtract).then_inc(less_ok, 1)
                        dve.wait_ge(less_ok, k1)
                        step(dve.tensor_tensor(here, top_new[u][:, :], top_new[u][:, :], ALU.max))

                    def take_sums(i, w, v, off):
                        k1, (s, it) = number(i, w, v, off + 1), slot_of(i, w, v, off)
                        dve.wait_ge(scale_ok, k1)
                        dve.tensor_tensor(part_sum[:, :, :], ps_acc[s % 2][:, 0:PW].rearrange("p (h d) -> p h d", h=HEADS),
                                          scale[s % 2][:, 1, :].unsqueeze(2).to_broadcast([P, HEADS, HDIM + 1]), ALU.mult).then_inc(acc_used, 1)

                    def add(i, w, v, off, b):
                        k1 = number(i, w, v, off + 1)
                        so_far = acc[:, ds(b, 1), :, :].rearrange("p a h d -> p (a h) d")
                        dve.wait_ge(acc_used, k1 + ACC_USED0)
                        dve.wait_ge(scaled, k1)
                        dve.tensor_tensor(so_far, so_far, part_sum[:, :, :], ALU.add).then_inc(added, 1)
                        dve.wait_ge(added, k1 + ADDED0)

                    def batch(i, w):
                        before = i * 2 + w - 1
                        for v in range(IV):
                            if v == 2 and is_batch(before):
                                dve.wait_ge(exp_ok, before + 1)
                            if is_item(number(i, w, v, -LAG)):
                                weigh(i, w, v, -LAG)
                            else:
                                dve.sem_inc(tick, 1)
                            if is_item(number(i, w, v, -LAG - 2)):
                                add_to = block_of(i, w, v, -LAG - 2)
                            if is_item(number(i, w, v, -LAG - 1)):
                                meet_in = block_of(i, w, v, -LAG - 1)
                            if is_item(number(i, w, v, -LAG - 2)):
                                take_sums(i, w, v, -LAG - 2)
                            if is_item(number(i, w, v, 2)):
                                compare(i, w, v, 2)
                            if is_item(number(i, w, v)):
                                left_and_right(i, w, v)
                                if v == 3:
                                    relate(i, w)
                            if is_item(number(i, w, v, -LAG - 2)):
                                add(i, w, v, -LAG - 2, add_to)
                            if is_item(number(i, w, v, -LAG - 1)):
                                meet(i, w, v, -LAG - 1, meet_in)
                            if v == IV - 1 and is_batch(i * 2 + w):
                                scores(i, w)
                            if v == 0 and is_batch(before):
                                tops(before, *((i, 0) if w else (i - 1, 1)))
                            if v == 1 and is_batch(before):
                                below_top(before, 1 - w)

                    for v in range(2):
                        compare(0, 0, v, 0)
                    all_batches(batch, dve, step, behind=1)
        edges_ctx.close()

        w13 = sb(ctx, "w13", [P, EXPERTS, KC * W13])
        gates = sb(ctx, "gates", [P, 2, BLOCKS])
        slots = sb(ctx, "slots", [P, 2, BLOCKS], I32)
        tile_expert = sb(ctx, "tile_expert", [1, TILES], I32)
        x2_ctx = ctx.enter_context(ExitStack())
        xall = sb(x2_ctx, "xall2", [P, BLOCKS, DIM])

        with ExitStack() as st:
            inv = sb(st, "inv", [P, BLOCKS, HEADS])
            stats = sb(st, "stats2", [P, BLOCKS, 6])
            tmp = sb(st, "tmp2", [P, BLOCKS, 2])
            eps = sb(st, "eps2", [P, 1])
            xn = sb(st, "xn2", [P, 2, DIM])
            xt = sb(st, "xt2", [P, 2, KC, P])
            ps_t = [ps(st, f"ps_t2{i}", [P, 512]) for i in range(2)]
            ps_l = [ps(st, f"ps_l{i}", [P, 512]) for i in range(2)]
            stats_ok, var_ok, std_ok, xn_ok, xt_ps, xt_sb, l_ps, l_sb, x2_out = map(
                sem, ("stats2_ok", "var2_ok", "std2_ok", "xn2_ok", "xt2_ps", "xt2_sb", "l_ps", "l_sb", "x2_out"))
            x_in2, x_zero = sem("x_in2"), sem("x_zero")

            with nc.Block() as block:
                @block.vector
                def _(dve):
                    step = dve_steps
                    dve.memset(xall[:, BLOCKS - 1, :], 0.0).then_inc(x_zero, 1)
                    step(dve.memset(eps[:, :], LN_EPS))
                    step(dve.tensor_scalar(inv[:, :, :], acc[:, 0:BLOCKS, :, HDIM], 0.5, None, ALU.max))
                    step(dve.reciprocal(inv[:, :, :], inv[:, :, :]))
                    with dve.Fori(0, BLOCKS // BC) as c:
                        step.loop(c, 2)
                        cb = ds(c * BC, BC)
                        rows4 = acc[:, cb, :, 0:HDIM]
                        step(dve.tensor_tensor(rows4, rows4, inv[:, cb, :].unsqueeze(3).to_broadcast([P, BC, HEADS, HDIM]), ALU.mult))
                        x4 = xall[:, cb, :].rearrange("p b (h d) -> p b h d", h=HEADS)
                        dve.wait_ge(x_in2, c * 16 + 32)
                        step(dve.tensor_tensor(x4, x4, rows4, ALU.add))
                        for j in range(BC):
                            dve.bn_stats(flat(stats[:, ds(c * BC + j, 1), :]), flat(xall[:, ds(c * BC + j, 1), :])).then_inc(stats_ok, 1)
                    step.end(BLOCKS // BC)
                    dve.wait_ge(stats_ok, BLOCKS)
                    join_stats(dve, step, stats, mv2, tmp, var_ok)
                    dve.wait_ge(std_ok, 1)
                    step(dve.reciprocal(rstd2[:, :], rstd2[:, :]))

                    def norm(b, u):
                        dve.tensor_scalar(xn[:, u, :], flat(xall[:, ds(b, 1), :]), mv2[:, ds(b, 1), 0],
                                          rstd2[:, ds(b, 1)], ALU.subtract, ALU.mult).then_inc(xn_ok, 1)

                    norm(0, 0)
                    norm(1, 1)
                    for u in range(2):
                        dve.wait_ge(xt_ps, u + 1)
                        norm(2 + u, u)
                    with dve.Fori(2, BLOCKS - 3, 2) as b:
                        for u in range(2):
                            dve.wait_ge(xt_ps, b + (u + 1))
                            norm(b + (2 + u), u)
                    dve.wait_ge(xt_ps, BLOCKS - 2)
                    norm(BLOCKS - 1, (BLOCKS - 1) % 2)

                @block.sync
                def _(sp):
                    sp.wait_ge(x_zero, 1)
                    sp.dma_start(xall[0:LAST, BLOCKS - 1, :], x[(BLOCKS - 1) * P:NODES, :]).then_inc(x_in2, 16)
                    for c in range(BLOCKS // BC):
                        lo, hi = c * BC, min((c + 1) * BC, BLOCKS - 1)
                        sp.dma_start(xall[:, lo:hi, :], x[lo * P:hi * P, :].rearrange("(b p) d -> p b d", p=P)).then_inc(x_in2, 16)
                        sp.wait_ge(x_in2, 16 * (c + 2))
                    sp.wait_ge(stats_ok, BLOCKS)
                    sp.dma_start(node_view(x2_dram), xall[:, :, :]).then_inc(x2_out, 16)
                    sp.wait_ge(x2_out, 16)

                @block.scalar
                def _(act):
                    act.wait_ge(var_ok, 1)
                    act.activation(rstd2[:, :], mv2[:, :, 1], ACT.Sqrt, bias=eps[:, 0:1]).then_inc(std_ok, 1)

                    def copy_xt(b, u):
                        act.wait_ge(xt_ps, b + 1)
                        act.copy(xt[:, u, :, :], ps_t[u][:, 0:KC * P].rearrange("p (k n) -> p k n", k=KC)).then_inc(xt_sb, 1)

                    def copy_logits(b, u):
                        act.wait_ge(l_ps, b + 1)
                        act.copy(flat(lg[:, ds(b, 1), :]), ps_l[u][:, 0:EXPERTS]).then_inc(l_sb, 1)

                    copy_xt(0, 0)
                    copy_xt(1, 1)
                    with act.Fori(0, BLOCKS - 3, 2) as b:
                        for u in range(2):
                            copy_logits(b + u, u)
                            copy_xt(b + (2 + u), u)
                    copy_logits(BLOCKS - 3, 0)
                    copy_xt(BLOCKS - 1, 0)
                    copy_logits(BLOCKS - 2, 1)
                    copy_logits(BLOCKS - 1, 0)

                @block.tensor
                def _(pe):
                    def turn(b, u):
                        pe.wait_ge(xn_ok, b + 1)
                        for k in range(KC):
                            last = pe.transpose(ps_t[u][:, k * P:(k + 1) * P], xn[:, u, k * P:(k + 1) * P], ident[:, :])
                        last.then_inc(xt_ps, 1)

                    def logits(b, u):
                        pe.wait_ge(xt_sb, b + 1)
                        for k in range(KC):
                            last = pe.matmul(ps_l[u][:, 0:EXPERTS], xt[:, u, k, :], rt[:, k, :], start=(k == 0), stop=(k == KC - 1))
                        last.then_inc(l_ps, 1)

                    turn(0, 0)
                    turn(1, 1)
                    for b in range(2):
                        logits(b, b)
                        turn(2 + b, b)
                    with pe.Fori(2, BLOCKS - 3, 2) as b:
                        for u in range(2):
                            pe.wait_ge(l_sb, b + (u - 1))
                            logits(b + u, u)
                            turn(b + (2 + u), u)
                    for b in range(BLOCKS - 3, BLOCKS):
                        pe.wait_ge(l_sb, b - 1)
                        logits(b, b % 2)
                        if b + 2 < BLOCKS:
                            turn(b + 2, b % 2)
        clear_sems()

        weights_in = sem("weights_in")
        with ExitStack() as st:
            wide = [P, BLOCKS, EXPERTS]
            taken[0] = 0
            prob, hit, pick1, pick2, slot = (a.rearrange("p (b e) -> p b e", e=EXPERTS) for a in take(BLOCKS * EXPERTS, 5))
            total, seen, before = (a.rearrange("p (e b) -> p e b", e=EXPERTS) for a in take(BLOCKS * EXPERTS, 3))
            best = sb(st, "best", [P, 3, BLOCKS])
            den = sb(st, "den", [P, BLOCKS])
            rank = sb(st, "rank", [P, EXPERTS])
            real = sb(st, "real", [P, BLOCKS])
            spare = sb(st, "spare", [P, 2, BLOCKS])
            slots_f = sb(st, "slots_f", [P, 2, BLOCKS])
            upper = sb(st, "upper", [P, P])
            tiles_i = sb(st, "tiles_i", [P, EXPERTS], I32)
            tiles = sb(st, "tiles", [P, EXPERTS])
            tend = sb(st, "tend", [P, EXPERTS])
            tbase = sb(st, "tbase", [P, EXPERTS])
            tau = sb(st, "tau", [1, TILES])
            past = sb(st, "past", [1, TILES, EXPERTS])
            texp = sb(st, "texp", [1, TILES])
            row = take(DIM, BC)
            row_slot = [sb(st, f"row_slot{j}", [P, 2], I32) for j in range(BC)]
            ps_before = ps(st, "ps_before", [P, 512])
            ps_total = ps(st, "ps_total", [P, 512])
            r_const, less_ok, exp_done, pick_ok, rank_ps = map(sem, ("r_const", "less_best", "exp_done", "pick_ok", "rank_ps"))
            row_ok = sem("row_ok")
            sent = [sem(f"sent{j}") for j in range(BC)]

            def over(ap):
                return ap.unsqueeze(2).to_broadcast(wide)

            with nc.Block() as block:
                @block.gpsimd
                def _(pool):
                    pool.iota(rank[:, :], pattern=[[-1, EXPERTS]], base=EXPERTS, channel_multiplier=0,
                              allow_small_or_imprecise_dtypes=True).then_inc(r_const, 1)
                    pool.iota(real[:, :], pattern=[[P, BLOCKS]], base=0, channel_multiplier=1,
                              allow_small_or_imprecise_dtypes=True).then_inc(r_const, 1)
                    pool.iota(tau[:, :], pattern=[[1, TILES]], base=0, channel_multiplier=0,
                              allow_small_or_imprecise_dtypes=True).then_inc(r_const, 1)
                    pool.memset(upper[:, :], 1.0).then_inc(pool_step, 1)
                    pool.wait_ge(pool_step, 2)
                    pool.affine_select(out=upper[:, :], in_=upper[:, :], compare_op=ALU.is_ge, fill=0.0, base=-1,
                                       pattern=[[1, P]], channel_multiplier=-1).then_inc(r_const, 1)

                    with pool.Fori(0, BLOCKS // BC) as c:
                        for j in range(BC):
                            wait_apart(pool, row_ok, c * BC + (j + 1), tick)
                            for k in range(2):
                                pool.indirect_dma_start(slots_x, bass.IndirectOffsetOnAxis(ap=row_slot[j][:, k:k + 1], axis=0),
                                                        row[j][:, :], None).then_inc(sent[j], 16)
                    for j in range(BC):
                        pool.wait_ge(sent[j], 32 * (BLOCKS // BC))

                @block.sync
                def _(sp):
                    for e in range(EXPERTS):
                        sp.dma_start(w13[:, e, :], w13_t[e].rearrange("p k n -> p (k n)")).then_inc(weights_in, 16)
                    sp.wait_ge(weights_in, 16 * EXPERTS)

                @block.scalar
                def _(act):
                    act.wait_ge(less_ok, 1)
                    act.activation(prob[:, :, :], prob[:, :, :], ACT.Exp).then_inc(exp_done, 1)

                @block.tensor
                def _(pe):
                    pe.wait_ge(pick_ok, 1)
                    chosen = hit[:, :, :].rearrange("p b e -> p (b e)")
                    pe.matmul(ps_before[:, 0:BLOCKS * EXPERTS], upper[:, :], chosen, start=True, stop=True)
                    pe.matmul(ps_total[:, 0:BLOCKS * EXPERTS], ones[:, :], chosen, start=True, stop=True).then_inc(rank_ps, 1)

                @block.vector
                def _(dve):
                    step = dve_steps
                    dve.wait_ge(r_const, 4)
                    step(dve.tensor_reduce(den[:, :], lg[:, :, :], AX.X, ALU.max))
                    dve.tensor_tensor(prob[:, :, :], lg[:, :, :], over(den[:, :]), ALU.subtract).then_inc(less_ok, 1)
                    dve.wait_ge(exp_done, 1)
                    step(dve.tensor_reduce(den[:, :], prob[:, :, :], AX.X, ALU.add))
                    step(dve.reciprocal(den[:, :], den[:, :]))
                    step(dve.tensor_tensor(prob[:, :, :], prob[:, :, :], over(den[:, :]), ALU.mult))

                    def pick(n, out):
                        step(dve.tensor_reduce(best[:, n, :], prob[:, :, :], AX.X, ALU.max))
                        step(dve.tensor_tensor(hit[:, :, :], prob[:, :, :], over(best[:, n, :]), ALU.is_equal))
                        step(dve.tensor_tensor(hit[:, :, :], hit[:, :, :], rank[:, :].unsqueeze(1).to_broadcast(wide), ALU.mult))
                        step(dve.tensor_reduce(best[:, 2, :], hit[:, :, :], AX.X, ALU.max))
                        step(dve.tensor_tensor(out[:, :, :], hit[:, :, :], over(best[:, 2, :]), ALU.is_equal))

                    pick(0, pick1)
                    step(dve.scalar_tensor_tensor(prob[:, :, :], pick1[:, :, :], -2.0, prob[:, :, :], ALU.mult, ALU.add))
                    pick(1, pick2)
                    step(dve.scalar_tensor_tensor(den[:, :], best[:, 0, :], 1e-9, best[:, 1, :], ALU.add, ALU.add))
                    step(dve.reciprocal(den[:, :], den[:, :]))
                    for n in range(2):
                        step(dve.tensor_tensor(gates[:, n, :], best[:, n, :], den[:, :], ALU.mult))
                    step(dve.tensor_scalar(real[:, :], real[:, :], float(NODES), None, ALU.is_lt))
                    for n in range(2):
                        step(dve.tensor_scalar(spare[:, n, :], real[:, :], -1.0, 1.0, ALU.mult, ALU.add))
                        step(dve.tensor_scalar(den[:, 0:1], part[:, :], float((TILES + n) * P), None, ALU.add))
                        step(dve.tensor_scalar(spare[:, n, :], spare[:, n, :], den[:, 0:1], None, ALU.mult))
                    step(dve.tensor_tensor(hit[:, :, :], pick1[:, :, :], pick2[:, :, :], ALU.add))
                    dve.tensor_tensor(hit[:, :, :], hit[:, :, :], over(real[:, :]), ALU.mult).then_inc(pick_ok, 1)
                    dve.wait_ge(rank_ps, 1)
                    step(dve.tensor_copy(total[:, :, :], ps_total[:, 0:BLOCKS * EXPERTS].rearrange("p (b e) -> p e b", e=EXPERTS)))
                    step(dve.memset(before[:, :, :], 1.0))
                    for e in range(EXPERTS):
                        step(dve.tensor_tensor_scan(seen[:, e, :], before[:, e, :], total[:, e, :], 0.0, ALU.mult, ALU.add))
                    step(dve.tensor_tensor(before[:, :, :], seen[:, :, :], total[:, :, :], ALU.subtract))
                    step(dve.tensor_scalar(tiles_i[:, :], seen[:, :, BLOCKS - 1], float(P - 1), None, ALU.add))
                    step(dve.tensor_scalar(tiles_i[:, :], tiles_i[:, :], P.bit_length() - 1, None, ALU.arith_shift_right))
                    step(dve.tensor_copy(tiles[:, :], tiles_i[:, :]))
                    step(dve.memset(tbase[:, :], 1.0))
                    step(dve.tensor_tensor_scan(tend[:, :], tbase[:, :], tiles[:, :], 0.0, ALU.mult, ALU.add))
                    step(dve.tensor_tensor(tbase[:, :], tend[:, :], tiles[:, :], ALU.subtract))
                    step(dve.scalar_tensor_tensor(slot[:, :, :], tbase[:, :].unsqueeze(1).to_broadcast(wide), float(P),
                                                  ps_before[:, 0:BLOCKS * EXPERTS].rearrange("p (b e) -> p b e", e=EXPERTS),
                                                  ALU.mult, ALU.add))
                    step(dve.tensor_tensor(slot[:, :, :], slot[:, :, :], before[:, :, :].rearrange("p e b -> p b e"), ALU.add))
                    for n, choice in enumerate((pick1, pick2)):
                        step(dve.tensor_tensor(choice[:, :, :], choice[:, :, :], slot[:, :, :], ALU.mult))
                        step(dve.tensor_reduce(slots_f[:, n, :], choice[:, :, :], AX.X, ALU.add))
                        step(dve.tensor_tensor(slots_f[:, n, :], slots_f[:, n, :], real[:, :], ALU.mult))
                        step(dve.tensor_tensor(slots_f[:, n, :], slots_f[:, n, :], spare[:, n, :], ALU.add))
                    step(dve.tensor_copy(slots[:, :, :], slots_f[:, :, :]))
                    step(dve.tensor_tensor(past[:, :, :], tau[:, :].unsqueeze(2).to_broadcast([1, TILES, EXPERTS]),
                                           tend[0:1, :].unsqueeze(1).to_broadcast([1, TILES, EXPERTS]), ALU.is_ge))
                    step(dve.tensor_reduce(texp[:, :], past[:, :, :], AX.X, ALU.add))
                    step(dve.tensor_scalar(tile_expert[:, :], texp[:, :], float(EXPERTS - 1), None, ALU.min))

                    def row_of(b, j):
                        dve.tensor_scalar(row[j][:, :], flat(xall[:, ds(b, 1), :]), mv2[:, ds(b, 1), 0], rstd2[:, ds(b, 1)],
                                          ALU.subtract, ALU.mult)
                        dve.tensor_copy(row_slot[j][:, :], slots[:, :, ds(b, 1)].rearrange("p k b -> p (k b)")).then_inc(row_ok, 1)

                    for j in range(BC):
                        row_of(j, j)
                    with dve.Fori(1, BLOCKS // BC) as c:
                        for j in range(BC):
                            dve.wait_ge(sent[j], c * 32)
                            row_of(c * BC + j, j)

        x2_ctx.close()

        UT = 3
        assert TILES % UT == 0
        taken[0] = 0
        xs, xt, hs, ht, yo = take(DIM, UT), take(KC * P, UT), take(HID, UT), take(HCH * P, UT), take(DIM, UT)
        HCUT = HCH // 2
        with ExitStack() as st:
            w2s = sb(st, "w2s", [P, EXPERTS, HCH * DIM])
            w2s_in = sem("w2s_in")
            ps_h = [ps(st, f"ps_h{n}", [P, 512]) for n in range(4)]
            ps_g = ps(st, "ps_g", [P, 1024])
            ps_t = ps(st, "ps_t3", [P, 512])
            ps_y = ps(st, "ps_y3", [P, 512])
            xs_in = [sem(f"xs_in{v}") for v in range(UT)]
            y_out = [sem(f"y_out{v}") for v in range(UT)]
            xt_ps, xt_sb, h1_ps, h3_ps, silu_ok, h_ok, ht_ps, ht_a, ht_d, y_ps, y_sb = map(sem, (
                "xt3_ps", "xt3_sb", "h1_ps", "h3_ps", "silu_ok", "h_ok", "ht_ps", "ht_a", "ht_d", "y_ps", "y_sb"))

            def after(eng, s, value):
                if not isinstance(value, int) or value > 0:
                    eng.wait_ge(s, value)

            def tiles_in_turn(eng, body):
                last = TILES // UT - 1
                for v in range(UT):
                    body(0, v)
                with eng.Fori(1, last) as i:
                    for v in range(UT):
                        body(i, v)
                for v in range(UT):
                    body(last, v)

            def ht_at(c):
                return c // HCUT * 512 + c % HCUT * P

            with nc.Block() as block:
                @block.sync
                def _(sp):
                    def load(i, v):
                        after(sp, xt_ps, (i - 1) * UT + v + 1)
                        sp.dma_start(xs[v], slots_x[ds((i * UT + v) * P, P), :]).then_inc(xs_in[v], 16)
                    for v in range(UT):
                        load(0, v)
                    for e in range(EXPERTS):
                        sp.dma_start(w2s[:, e, :], w2_t[e].rearrange("p k n -> p (k n)")).then_inc(w2s_in, 16)
                    with sp.Fori(1, TILES // UT) as i:
                        for v in range(UT):
                            wait_apart(sp, xt_ps, (i - 1) * UT + (v + 1), tick)
                            sp.dma_start(xs[v], slots_x[ds((i * UT + v) * P, P), :]).then_inc(xs_in[v], 16)

                @block.gpsimd
                def _(pool):
                    with pool.Fori(0, TILES // UT) as i:
                        for v in range(UT):
                            wait_apart(pool, y_sb, i * UT + (v + 1), tick)
                            pool.dma_start(slots_y[ds((i * UT + v) * P, P), :], yo[v]).then_inc(y_out[v], 16)
                    for v in range(UT):
                        pool.wait_ge(y_out[v], 16 * (TILES // UT))

                @block.scalar
                def _(act):
                    def copy_xt(i, v):
                        act.wait_ge(xt_ps, i * UT + (v + 1))
                        act.copy(xt[v], ps_t[:, 0:KC * P]).then_inc(xt_sb, 1)

                    def finish(i, v):
                        i, v = (i, v - 1) if v else (i - 1, UT - 1)
                        k = i * UT + v
                        act.wait_ge(ht_ps, k + 1)
                        act.copy(ht[v][:, 0:HCUT * P], ps_g[:, 0:HCUT * P]).then_inc(ht_a, 1)
                        return lambda: (act.wait_ge(y_ps, k + 1), after(act, y_out[v], i * 16),
                                        act.copy(yo[v], ps_y[:, 0:DIM]).then_inc(y_sb, 1))

                    def tile(i, v):
                        k = i * UT + v
                        act.wait_ge(h1_ps, k + 1)
                        after(act, ht_ps, k - UT + 1)
                        for n in range(2):
                            last = act.activation(hs[v][:, n * HALF:(n + 1) * HALF], ps_h[n][:, 0:HALF], ACT.Silu)
                        last.then_inc(silu_ok, 1)
                        first_tile = isinstance(i, int) and i == 0 and v == 0
                        last_tile = isinstance(i, int) and k == TILES - 1
                        y_copy = None if first_tile else finish(i, v)
                        if not last_tile:
                            copy_xt(*((i, v + 1) if v + 1 < UT else (i + 1, 0)))
                        if y_copy:
                            y_copy()

                    copy_xt(0, 0)
                    tiles_in_turn(act, tile)
                    finish(TILES // UT, 0)()

                @block.vector
                def _(dve):
                    def finish(i, v):
                        i, v = (i, v - 1) if v else (i - 1, UT - 1)
                        dve.wait_ge(ht_ps, i * UT + (v + 1))
                        n = HCH - 1 - HCUT
                        dve.tensor_copy(ht[v][:, HCUT * P:(HCH - 1) * P], ps_g[:, 512:512 + n * P])
                        dve.tensor_copy(ht[v][0:HLAST, (HCH - 1) * P:HCH * P],
                                        ps_g[0:HLAST, 512 + n * P:512 + (n + 1) * P]).then_inc(ht_d, 1)

                    def tile(i, v):
                        k = i * UT + v
                        if not (isinstance(i, int) and k == 0):
                            finish(i, v)
                        dve.wait_ge(silu_ok, k + 1)
                        dve.wait_ge(h3_ps, k + 1)
                        for n in range(2):
                            cols = hs[v][:, n * HALF:(n + 1) * HALF]
                            last = dve.tensor_tensor(cols, cols, ps_h[2 + n][:, 0:HALF], ALU.mult)
                        last.then_inc(h_ok, 1)

                    tiles_in_turn(dve, tile)
                    finish(TILES // UT, 0)

                @block.tensor
                def _(pe):
                    def turn(i, v):
                        pe.wait_ge(xs_in[v], i * 16 + 16)
                        for k in range(KC):
                            last = pe.transpose(ps_t[:, k * P:(k + 1) * P], xs[v][:, k * P:(k + 1) * P], ident[:, :])
                        last.then_inc(xt_ps, 1)

                    def up(e, v, m, done):
                        for half in range(2):
                            for k in range(KC):
                                at = k * W13 + m * HID + half * HALF
                                last = pe.matmul(ps_h[2 * m + half][:, 0:HALF], xt[v][:, k * P:(k + 1) * P],
                                                 flat(w13[:, ds(e, 1), at:at + HALF]), start=(k == 0), stop=(k == KC - 1))
                        last.then_inc(done, 1)

                    def turn_h(v):
                        for c in range(HCH):
                            w = min(P, HID - c * P)
                            last = pe.transpose(ps_g[0:w, ht_at(c):ht_at(c) + P], hs[v][:, c * P:c * P + w], ident[:, :])
                        last.then_inc(ht_ps, 1)

                    def down(e, v):
                        for c in range(HCH):
                            w = min(P, HID - c * P)
                            last = pe.matmul(ps_y[:, 0:DIM], ht[v][0:w, c * P:(c + 1) * P],
                                             flat(w2s[0:w, ds(e, 1), c * DIM:(c + 1) * DIM]), start=(c == 0), stop=(c == HCH - 1))
                        last.then_inc(y_ps, 1)

                    def expert(k):
                        return pe.value_load(tile_expert[0:1, ds(k, 1)], min_val=0, max_val=EXPERTS - 1)

                    def tile(i, v):
                        k = i * UT + v
                        first_tile = isinstance(i, int) and k == 0
                        last_tile = isinstance(i, int) and k == TILES - 1
                        e = expert(k)
                        pe.wait_ge(xt_sb, k + 1)
                        after(pe, silu_ok, k)
                        up(e, v, 0, h1_ps)
                        u = (v - 1) % UT
                        if not first_tile:
                            pe.wait_ge(h_ok, k)
                            after(pe, ht_a, k - 1)
                            after(pe, ht_d, k - 1)
                            turn_h(u)
                        if not last_tile:
                            turn(*((i, v + 1) if v + 1 < UT else (i + 1, 0)))
                        up(e, v, 1, h3_ps)
                        if not first_tile:
                            e_before = expert(k - 1)
                            pe.wait_ge(ht_a, k)
                            pe.wait_ge(ht_d, k)
                            after(pe, y_sb, k - 1)
                            if isinstance(i, int) and k == 1:
                                pe.wait_ge(w2s_in, 16 * EXPERTS)
                            down(e_before, u)

                    turn(0, 0)
                    tiles_in_turn(pe, tile)
                    k = TILES
                    pe.wait_ge(h_ok, k)
                    pe.wait_ge(ht_a, k - 1)
                    pe.wait_ge(ht_d, k - 1)
                    turn_h((k - 1) % UT)
                    e_last = expert(k - 1)
                    pe.wait_ge(ht_a, k)
                    pe.wait_ge(ht_d, k)
                    pe.wait_ge(y_sb, k - 1)
                    down(e_last, (k - 1) % UT)

        UB = 6
        FULL = BLOCKS - 1
        assert FULL % UB == 0
        taken[0] = 0
        ya, yb, xo = take(DIM, UB), take(DIM, UB), take(DIM, UB)
        with ExitStack() as st:
            pair = [sb(st, f"pair{v}", [P, 2], I32) for v in range(UB)]
            y_in, x_in3, o_out = ([sem(f"{n}{v}") for v in range(UB)] for n in ("y_in", "x_in3_", "o_out"))
            pair_ok, mix1, mix2 = sem("pair_ok"), sem("mix1"), sem("mix2")

            def in_turn(eng, body):
                for v in range(UB):
                    body(0, v, v)
                with eng.Fori(1, FULL // UB) as i:
                    for v in range(UB):
                        body(i, v, i * UB + v)
                body(FULL // UB, 0, FULL)

            with nc.Block() as block:
                @block.gpsimd
                def _(pool):
                    def fetch(i, v, b):
                        after(pool, mix2, b - UB + 1)
                        pool.tensor_copy(pair[v][:, :], slots[:, :, ds(b, 1)].rearrange("p k b -> p (k b)")).then_inc(pair_ok, 1)
                        wait_apart(pool, pair_ok, b + 1, tick)
                        for n, y in enumerate((ya, yb)):
                            pool.indirect_dma_start(y[v], None, slots_y,
                                                    bass.IndirectOffsetOnAxis(ap=pair[v][:, n:n + 1], axis=0)).then_inc(y_in[v], 16)
                    in_turn(pool, fetch)

                @block.sync
                def _(sp):
                    def load(i, v, b):
                        if not (isinstance(i, int) and i == 0):
                            wait_apart(sp, o_out[v], i * 16, tick)
                        sp.dma_start(xo[v], x2_dram[ds(b * P, P), :]).then_inc(x_in3[v], 16)
                    in_turn(sp, load)

                @block.vector
                def _(dve):
                    def mix(i, v, b):
                        dve.wait_ge(y_in[v], i * 32 + 32)
                        dve.wait_ge(x_in3[v], i * 16 + 16)
                        dve.scalar_tensor_tensor(xo[v], ya[v], flat(gates[:, 0:1, ds(b, 1)]), xo[v], ALU.mult, ALU.add).then_inc(mix1, 1)
                        dve.wait_ge(mix1, b + 1)
                        dve.scalar_tensor_tensor(xo[v], yb[v], flat(gates[:, 1:2, ds(b, 1)]), xo[v], ALU.mult, ALU.add).then_inc(mix2, 1)
                    in_turn(dve, mix)

                @block.scalar
                def _(act):
                    def store(i, v, b):
                        if isinstance(b, int) and b == FULL:
                            act.wait_ge(mix2, b + 1)
                            act.dma_start(out[FULL * P:NODES, :], xo[v][0:LAST, :]).then_inc(o_out[v], 16)
                        else:
                            wait_apart(act, mix2, b + 1, tick)
                            act.dma_start(out[ds(b * P, P), :], xo[v]).then_inc(o_out[v], 16)
                    in_turn(act, store)
                    for v in range(UB):
                        act.wait_ge(o_out[v], 16 * (FULL // UB + (v == 0)))


_INS = ['x', 'src', 'dst', 'edge_attr_16', 'edge_attr_4', 'L0_gnn_W_n', 'L0_gnn_attn_l', 'L0_gnn_attn_r', 'L0_gnn_attn_m',
        'L0_ffn_router_w', 'L0_ffn_w1', 'L0_ffn_w2', 'L0_ffn_w3']


def kernel(**inputs):
    import numpy as _np
    import concourse.bacc as _bacc
    from concourse import mybir as _mybir
    from concourse.bass_utils import run_bass_kernel_spmd as _run

    nc = _bacc.Bacc("TRN2", target_bir_lowering=False, num_devices=1)
    arrays, args = {}, []
    for name in _INS:
        a = _np.ascontiguousarray(inputs[name])
        arrays[f"in_{name}_dram"] = a
        args.append(nc.dram_tensor(f"in_{name}_dram", a.shape, _mybir.dt.from_np(a.dtype), kind="ExternalInput").ap())
    args.append(nc.dram_tensor("out_0_dram", (NODES, DIM), F32, kind="ExternalOutput").ap())
    gnn_moe_kernel(nc, *args)
    r = _run(nc, [arrays], core_ids=[0])
    return r.results[0]["out_0_dram"]
```
